# Optimizing a Trainium2 kernel written in Bass

```python
import numpy as np
import jax
import jax.numpy as jnp

def _softmax(x, axis=-1):
    return jax.nn.softmax(x, axis=axis)

def _gelu(x):
    return jax.nn.gelu(x, approximate=True)

def _silu(x):
    return jax.nn.silu(x)

def _sigmoid(x):
    return jax.nn.sigmoid(x)

def _layernorm(x, axis=-1, eps=1e-05):
    m = jnp.mean(x, axis=axis, keepdims=True)
    v = jnp.var(x, axis=axis, keepdims=True)
    return (x - m) / jnp.sqrt(v + eps)

def _scatter_add(tgt, idx, src, axis=0):
    return tgt.at[idx].add(src)

def _segment_sum(src, seg, n):
    return jax.ops.segment_sum(src, seg, n)
kernel_name = 'mk_seq_preln_d1_jaxref_r4_e22d92'

def setup_inputs(seed: int=0):
    np.random.seed(seed)
    _w = jnp.asarray

    def _L0_attn_setup():
        import jax, jax.numpy as jnp
        import numpy as np
        NUM_HEADS = 16
        EMBED_DIM = 256

        def _linear_attention(x, Wq, bq, Wk, bk, Wv, bv, Wo, bo):
            B, S, D = x.shape
            H = NUM_HEADS
            hd = D // H
            v = (x @ Wv + bv).reshape(B, S, H, hd)
            q = (x @ Wq + bq).reshape(B, S, H, hd)
            k = (x @ Wk + bk).reshape(B, S, H, hd)
            q = jax.nn.elu(q) + 1.0
            k = jax.nn.elu(k) + 1.0
            qT = q.transpose(1, 0, 2, 3)
            kT = k.transpose(1, 0, 2, 3)
            vT = v.transpose(1, 0, 2, 3)
            s0 = jnp.zeros((B, H, hd, hd), dtype=x.dtype)
            z0 = jnp.zeros((B, H, hd), dtype=x.dtype)

            def step(carry, qkv):
                s, z = carry
                q_i, k_i, v_i = qkv
                s = s + jnp.einsum('bhd,bhm->bhdm', k_i, v_i)
                z = z + k_i
                qs = jnp.einsum('bhd,bhdm->bhm', q_i, s)
                qz = jnp.einsum('bhd,bhd->bh', q_i, z)[..., None]
                return ((s, z), qs / (qz + 1e-06))
            (_, _), values = jax.lax.scan(step, (s0, z0), (qT, kT, vT))
            values = values.transpose(1, 0, 2, 3).reshape(B, S, D)
            return values @ Wo + bo
        key = jax.random.key(seed)
        ks = jax.random.split(key, 6)
        B, S, D = (4, 512, EMBED_DIM)
        sc = 1.0 / np.sqrt(D)
        return {'x': jax.random.normal(ks[0], (B, S, D), dtype=jnp.float32), 'mask': jnp.ones((B, S), dtype=jnp.int32), 'Wq': jax.random.normal(ks[1], (D, D), dtype=jnp.float32) * sc, 'bq': jnp.zeros((D,), dtype=jnp.float32), 'Wk': jax.random.normal(ks[2], (D, D), dtype=jnp.float32) * sc, 'bk': jnp.zeros((D,), dtype=jnp.float32), 'Wv': jax.random.normal(ks[3], (D, D), dtype=jnp.float32) * sc, 'bv': jnp.zeros((D,), dtype=jnp.float32), 'Wo': jax.random.normal(ks[4], (D, D), dtype=jnp.float32) * sc, 'bo': jnp.zeros((D,), dtype=jnp.float32)}
    _L0_attn_in = _L0_attn_setup()

    def _L0_ffn_setup():
        import jax, jax.numpy as jnp
        import numpy as np
        S, B, H, F, E, K = (512, 2, 256, 512, 8, 2)

        def _moe_forward(hidden_states, router_w, w1, b1, w2, b2):
            s, b, h = hidden_states.shape
            T = s * b
            x = hidden_states.reshape(T, h)
            logits = jnp.einsum('th,eh->te', x, router_w)
            topk_logits, topk_idx = jax.lax.top_k(logits, K)
            probs = jax.nn.softmax(topk_logits, axis=-1)
            combine = jnp.zeros((T, E), dtype=x.dtype)
            combine = combine.at[jnp.arange(T)[:, None], topk_idx].add(probs.astype(x.dtype))
            hmid = jnp.einsum('th,efh->etf', x, w1) + b1[:, None, :]
            hmid = jax.nn.gelu(hmid, approximate=False)
            y = jnp.einsum('etf,ehf->eth', hmid, w2) + b2[:, None, :]
            out = jnp.einsum('eth,te->th', y, combine)
            return out.reshape(s, b, h)
        key = jax.random.key(seed)
        ks = jax.random.split(key, 6)
        std = 0.02
        return {'hidden_states': jax.random.normal(ks[0], (S, B, H), dtype=jnp.float32), 'router_w': jax.random.normal(ks[1], (E, H), dtype=jnp.float32) * std, 'w1': jax.random.normal(ks[2], (E, F, H), dtype=jnp.float32) * (1.0 / np.sqrt(H)), 'b1': jnp.zeros((E, F), dtype=jnp.float32), 'w2': jax.random.normal(ks[3], (E, H, F), dtype=jnp.float32) * (1.0 / np.sqrt(F)), 'b2': jnp.zeros((E, H), dtype=jnp.float32)}
    _L0_ffn_in = _L0_ffn_setup()
    _d = {'L0_attn_x': _L0_attn_in['x'], 'L0_attn_mask': _L0_attn_in['mask'], 'L0_attn_Wq': _L0_attn_in['Wq'], 'L0_attn_bq': _L0_attn_in['bq'], 'L0_attn_Wk': _L0_attn_in['Wk'], 'L0_attn_bk': _L0_attn_in['bk'], 'L0_attn_Wv': _L0_attn_in['Wv'], 'L0_attn_bv': _L0_attn_in['bv'], 'L0_attn_Wo': _L0_attn_in['Wo'], 'L0_attn_bo': _L0_attn_in['bo'], 'L0_ffn_router_w': _L0_ffn_in['router_w'], 'L0_ffn_w1': _L0_ffn_in['w1'], 'L0_ffn_b1': _L0_ffn_in['b1'], 'L0_ffn_w2': _L0_ffn_in['w2'], 'L0_ffn_b2': _L0_ffn_in['b2']}
    _x0 = _d['L0_attn_x']
    _d['L0_attn_x'] = jax.random.normal(jax.random.fold_in(jax.random.key(seed), 1), (4, 2048, 256), dtype=_x0.dtype)
    del _x0
    return _d

def reference(L0_attn_x, L0_attn_mask, L0_attn_Wq, L0_attn_bq, L0_attn_Wk, L0_attn_bk, L0_attn_Wv, L0_attn_bv, L0_attn_Wo, L0_attn_bo, L0_ffn_router_w, L0_ffn_w1, L0_ffn_b1, L0_ffn_w2, L0_ffn_b2):

    def _L0_attn_ref(x, mask, Wq, bq, Wk, bk, Wv, bv, Wo, bo):
        import jax, jax.numpy as jnp
        import numpy as np
        NUM_HEADS = 16
        EMBED_DIM = 256

        def _linear_attention(x, Wq, bq, Wk, bk, Wv, bv, Wo, bo):
            B, S, D = x.shape
            H = NUM_HEADS
            hd = D // H
            v = (x @ Wv + bv).reshape(B, S, H, hd)
            q = (x @ Wq + bq).reshape(B, S, H, hd)
            k = (x @ Wk + bk).reshape(B, S, H, hd)
            q = jax.nn.elu(q) + 1.0
            k = jax.nn.elu(k) + 1.0
            qT = q.transpose(1, 0, 2, 3)
            kT = k.transpose(1, 0, 2, 3)
            vT = v.transpose(1, 0, 2, 3)
            s0 = jnp.zeros((B, H, hd, hd), dtype=x.dtype)
            z0 = jnp.zeros((B, H, hd), dtype=x.dtype)

            def step(carry, qkv):
                s, z = carry
                q_i, k_i, v_i = qkv
                s = s + jnp.einsum('bhd,bhm->bhdm', k_i, v_i)
                z = z + k_i
                qs = jnp.einsum('bhd,bhdm->bhm', q_i, s)
                qz = jnp.einsum('bhd,bhd->bh', q_i, z)[..., None]
                return ((s, z), qs / (qz + 1e-06))
            (_, _), values = jax.lax.scan(step, (s0, z0), (qT, kT, vT))
            values = values.transpose(1, 0, 2, 3).reshape(B, S, D)
            return values @ Wo + bo
        return _linear_attention(x, Wq, bq, Wk, bk, Wv, bv, Wo, bo)

    def _L0_ffn_ref(hidden_states, router_w, w1, b1, w2, b2):
        import jax, jax.numpy as jnp
        import numpy as np
        S, B, H, F, E, K = (512, 2, 256, 512, 8, 2)

        def _moe_forward(hidden_states, router_w, w1, b1, w2, b2):
            s, b, h = hidden_states.shape
            T = s * b
            x = hidden_states.reshape(T, h)
            logits = jnp.einsum('th,eh->te', x, router_w)
            topk_logits, topk_idx = jax.lax.top_k(logits, K)
            probs = jax.nn.softmax(topk_logits, axis=-1)
            combine = jnp.zeros((T, E), dtype=x.dtype)
            combine = combine.at[jnp.arange(T)[:, None], topk_idx].add(probs.astype(x.dtype))
            hmid = jnp.einsum('th,efh->etf', x, w1) + b1[:, None, :]
            hmid = jax.nn.gelu(hmid, approximate=False)
            y = jnp.einsum('etf,ehf->eth', hmid, w2) + b2[:, None, :]
            out = jnp.einsum('eth,te->th', y, combine)
            return out.reshape(s, b, h)
        return _moe_forward(hidden_states, router_w, w1, b1, w2, b2)
    x = L0_attn_x
    x = x + _L0_attn_ref(_layernorm(x, axis=-1), L0_attn_mask, L0_attn_Wq, L0_attn_bq, L0_attn_Wk, L0_attn_bk, L0_attn_Wv, L0_attn_bv, L0_attn_Wo, L0_attn_bo)
    x = x + _L0_ffn_ref(_layernorm(x, axis=-1), L0_ffn_router_w, L0_ffn_w1, L0_ffn_b1, L0_ffn_w2, L0_ffn_b2)
    return x

_drawn_inputs = setup_inputs


def setup_inputs(seed=0):
    import zlib

    import numpy as np

    out = dict(_drawn_inputs(seed))
    spreads = {'L0_attn_bq': (0.0, 1.462),
     'L0_attn_bk': (0.0, 2.0),
     'L0_attn_bv': (0.0, 0.1),
     'L0_attn_bo': (0.0, 0.1),
     'L0_ffn_b1': (0.0, 0.1),
     'L0_ffn_b2': (0.0, 0.1)}
    factors = {}
    for name, (base, spread) in spreads.items():
        noise = np.random.default_rng([zlib.crc32(name.encode()), seed]).standard_normal(out[name].shape)
        drawn = base * np.exp(spread * noise) if base else spread * noise
        out[name] = jnp.asarray(drawn.astype(out[name].dtype))
    for name, factor in factors.items():
        out[name] = (out[name] * factor).astype(out[name].dtype)
    return out
```

```python
import math
from contextlib import ExitStack

import concourse.bass as bass
from concourse import mybir

F32, F16, BF16 = mybir.dt.float32, mybir.dt.float16, mybir.dt.bfloat16
I32, U32 = mybir.dt.int32, mybir.dt.uint32
ACT = mybir.ActivationFunctionType
ALU = mybir.AluOpType
AX = mybir.AxisListType

P = 128
B, S, D = 4, 2048, 256
H, HD = 16, 16
E, F = 8, 512
T = B * S
C = 128
STEPS = S // C
KC = D // P
VC = HD + 1
HC = H // KC
PAIRS = H // 2
STACK = 3 * 2 * HD
FC = F // P
MT = 256
CAP = T + MT
NT = (2 * T + E * (MT - 1)) // MT
DUMMY = E * CAP
ROWS = DUMMY + E * MT
WS = 16.0
QS = 0.5
EPS = 1e-5
DEN_EPS = 1e-6 * QS * QS

C_IDENT, C_BLOCK, C_IOTA8, C_CAPS, C_TRI8, C_TILES = 0, 128, 128 + KC * HC * VC, 408, 416, 480
C_POW, C_LN, C_ROW0, C_ROW1, C_END = 552, 556, 557, 558, 560
H_TRI, H_ONES, H_END = 0, 128, 256
B_IDENT, B_MASK, B_END = 0, P, P + C


def constants():
    import numpy as np

    p = np.arange(P)
    f = np.zeros((P, C_END), np.float32)
    f[:, C_IDENT:C_IDENT + P] = np.eye(P)
    f[:, C_BLOCK:C_BLOCK + KC * HC * VC] = np.tile(np.repeat(p[:, None] // HD == np.arange(HC), VC, axis=1), (1, KC))
    f[:, C_IOTA8:C_IOTA8 + E] = np.arange(E)
    f[:, C_CAPS:C_CAPS + E] = np.arange(E) * CAP
    f[:, C_TRI8:C_TRI8 + E * E] = (np.arange(E)[:, None] >= np.arange(E)).reshape(-1)
    f[:, C_TILES:C_TILES + NT] = np.arange(NT)
    f[:, C_POW:C_POW + B] = -0.5
    f[:, C_LN] = math.log(QS)
    f[:, C_ROW0], f[:, C_ROW1] = p, p + P
    h = np.zeros((P, H_END), np.float16)
    h[:, H_TRI:H_TRI + P] = p[:, None] < p
    h[:, H_ONES:] = 1
    b = np.zeros((P, B_END), np.float32)
    b[:, B_IDENT:B_IDENT + P] = np.eye(P)
    b[:, B_MASK:] = np.where(p[:, None] <= p, 0.0, -1e30)
    return f, h, b


def build(nc, x, wqkvo, bqk, bv, bo, rw, w1, b1, w2, b2, cf, ch, cb, out):
    qk_dram = nc.dram_tensor("qk_parts", (2, 2, 4, P, B * C), F16, kind="Internal").ap()
    x1_dram = nc.dram_tensor("x1_rows", (T, D), F32, kind="Internal").ap()
    xg_dram = nc.dram_tensor("expert_in", (ROWS, D), F32, kind="Internal").ap()
    y_dram = nc.dram_tensor("expert_out", (NT * MT, D), F32, kind="Internal").ap()
    x_steps = x.rearrange("(b i p) d -> i p b d", b=B, p=C)
    x1_steps = x1_dram.rearrange("(b i p) d -> i p b d", b=B, p=C)
    out_steps = out.rearrange("(b i p) d -> i p b d", b=B, p=C)

    with ExitStack() as ctx:
        def sem(name):
            return ctx.enter_context(nc.semaphore(name))

        def sb(name, shape, dt, where=ctx):
            return where.enter_context(nc.sbuf_tensor(name, shape, dt))

        def ps(name):
            return ctx.enter_context(nc.psum_tensor(name, [P, 512], F32))

        w1s = sb("w1s", [P, 2, E, KC, F], F16)
        was = sb("was", [P, 2, 4, KC, D], F16)
        cfs = sb("cfs", [P, C_END], F32)
        chs = sb("chs", [P, H_END], F16)
        cbs = sb("cbs", [P, B_END], BF16)
        b1s = sb("b1s", [P, E * FC], F32)
        slots = sb("slots", [P, STEPS, 2 * B], F32)
        y_slots = sb("y_slots", [P, STEPS, 2 * B], I32)
        probs = sb("probs", [P, STEPS, 2, B], F32)
        table = sb("table", [1, 2, NT], I32)
        zeros = sb("zeros", [P, D], F32)

        att = ExitStack()
        bqks = sb("bqks", [P, 4], F32, att)
        negb = sb("negb", [P, 4], F32, att)
        linb = sb("linb", [P, 4], F32, att)
        bvs = sb("bvs", [P, D], F32, att)
        bos = sb("bos", [P, D], F32, att)
        rws = sb("rws", [P, KC, E], F32, att)
        xs = sb("xs", [P, B, D], F32, att)
        xb = sb("xb", [P, 2, B, D], F32, att)
        st1 = sb("st1", [P, B, 6], F32, att)
        mv1 = sb("mv1", [P, B, 2], F32, att)
        ve1 = sb("ve1", [P, B], F32, att)
        rs1 = sb("rs1", [P, B], F32, att)
        st2 = sb("st2", [P, B, 6], F32, att)
        mv2 = sb("mv2", [P, B, 2], F32, att)
        ve2 = sb("ve2", [P, B], F32, att)
        rs2 = sb("rs2", [P, B], F32, att)
        xn = sb("xn", [P, B, D], F32, att)
        xT = sb("xT", [P, 2, KC, B * C], F16, att)
        et = sb("et", [P, 2, B * C], F32, att)
        lt = sb("lt", [P, 2, B * C], F32, att)
        qk = sb("qk", [P, 2, 4, B * C], F32, att)
        qkhl = sb("qkhl", [P, 2, 4, B * C], F16, att)
        kst = sb("kst", [P, 2, PAIRS, B * C], F16, att)
        qst = sb("qst", [P, 2, PAIRS, 2, B * C], F16, att)
        v = sb("v", [P, 2, B, H, VC], F32, att)
        vhl = sb("vhl", [P, 2, 2, B, H * VC], F16, att)
        kn = sb("kn", [P, B, D], F32, att)
        ahl = sb("ahl", [P, 2, 2, H * C], F16, att)
        state = sb("state", [P, B, KC, HC * VC], F32, att)
        ut = sb("ut", [P, KC * HC * VC], F32, att)
        rden = sb("rden", [P, 2, H], F32, att)
        at = sb("at", [P, D], F32, att)
        aT = sb("aT", [P, 2, KC, C], F16, att)
        x1 = sb("x1", [P, B, D], F32, att)
        xn2 = sb("xn2", [P, 2, B, D], F32, att)
        xn2T = sb("xn2T", [P, KC, C], F32, att)
        lg = sb("lg", [P, B, E], F32, att)
        mx = sb("mx", [P, B, 8], F32, att)
        ix = sb("ix", [P, B, 8], U32, att)
        ixf = sb("ixf", [P, B, 2], F32, att)
        pd = sb("pd", [P, 2, B], F32, att)
        oh = sb("oh", [P, B, 2, E], F32, att)
        cnt = sb("cnt", [P, B, E], F16, att)
        ctmp = sb("ctmp", [P, E], F16, att)
        carry = sb("carry", [P, E], F16, att)
        pos = sb("pos", [P, B, E], F32, att)
        sel = sb("sel", [P, B, 2, E], F32, att)
        slf = sb("slf", [P, 2 * B], F32, att)
        cur = sb("cur", [P, 2, 2 * B], I32, att)
        tiles_f = sb("tiles_f", [P, 4, E], F32, att)
        tiles_i = sb("tiles_i", [P, E], I32, att)
        tails_i = sb("tails_i", [P, 2, E], I32, att)
        att.close()
        past = et[0:1].rearrange("p a n -> p (a n)")[:, 0:NT * E].rearrange("p (t e) -> p t e", e=E)
        past_tiles = lt[0:1].rearrange("p a n -> p (a n)")[:, 0:NT * E].rearrange("p (t e) -> p t e", e=E)
        tails = xn[:, 2, 0:2 * E].rearrange("p (n e) -> p n e", n=2)
        behind, shift = [qk[:, 0, 2 * n:2 * n + 2].rearrange("p a n -> p (a n)")[:, 0:STEPS * 2 * B * (E - 1)]
                         .rearrange("p (s e) -> p s e", e=E - 1) for n in range(2)]
        spare = xn[0:1].rearrange("p b d -> p (b d)")
        upto = spare[:, 0:E * E].rearrange("p (a b) -> p a b", a=E)
        tj = spare[:, E * E:E * E + 4 * NT].rearrange("p (a t) -> p a t", a=4)

        moe = ExitStack()
        w2s = sb("w2s", [P, 2, E, FC, D], F16, moe)
        w2raw = sb("w2raw", [P, 2, 2, FC, D], F32, moe)
        b2s = sb("b2s", [P, E, D], F32, moe)
        xg = sb("xg", [P, 2, 2, D], F32, moe)
        gT = sb("gT", [P, 2, 2, KC * MT], F16, moe)
        g = sb("g", [P, 2, FC, MT], F32, moe)
        ghl = sb("ghl", [P, 2, 2, FC, MT], F16, moe)
        yt = sb("yt", [P, 2, 2, D], F32, moe)
        ya = sb("ya", [P, 2, 2 * B, D], F32, moe)
        xo = sb("xo", [P, 2, B, D], F32, moe)
        curg = sb("curg", [P, 2, 2 * B], I32, moe)
        moe.close()

        pF = [ps("pF0"), ps("pF1")]
        pS = [ps("pS0"), ps("pS1")]
        pO = ps("pO")
        pA = ps("pA")
        pU = ps("pU")
        pR = ps("pR")
        ident = cfs[:, C_IDENT:C_IDENT + P]
        block_mask = cfs[:, C_BLOCK:C_BLOCK + KC * HC * VC]
        ident16 = cbs[:, B_IDENT:B_IDENT + P]
        mask16 = cbs[:, B_MASK:B_END].unsqueeze(1).to_broadcast([P, 4, C])
        LOGITS, POS = KC * C, KC * C + B * E

        consts_in = sem("consts_in")
        CONSTS = 16 * 8
        passed = {nc.vector.engine: sem("passed_dve"), nc.gpsimd.engine: sem("passed_pool")}
        raw_in = sem("raw_in")
        w1_in = [sem("w1_in0"), sem("w1_in1")]
        wsplit_hi = sem("wsplit_hi")
        wsplit_lo = sem("wsplit_lo")
        bias_prep = sem("bias_prep")
        ones_set = sem("ones_set")
        zero_set = sem("zero_set")
        qst_zero = sem("qst_zero")
        pads_out = sem("pads_out")
        x_in = sem("x_in")
        ln1_st, ln1_mv, ln1_ve, ln1_rs = sem("ln1_st"), sem("ln1_mv"), sem("ln1_ve"), sem("ln1_rs")
        ln2_st, ln2_mv, ln2_ve, ln2_rs = sem("ln2_st"), sem("ln2_mv"), sem("ln2_ve"), sem("ln2_rs")
        xn_done, xb_done = sem("xn_done"), sem("xb_done")
        xT_ps, xT_hi, xT_lo = sem("xT_ps"), sem("xT_hi"), sem("xT_lo")
        qk_ps, qk_neg, qk_lin, qk_f = sem("qk_ps"), sem("qk_neg"), sem("qk_lin"), sem("qk_f")
        qk_hi, qk_lo, qk_out = sem("qk_hi"), sem("qk_lo"), sem("qk_out")
        stack_in = [sem("stack_in0"), sem("stack_in1")]
        v_ps, v_done, v_hi, v_lo = sem("v_ps"), sem("v_done"), sem("v_hi"), sem("v_lo")
        kn_ps, kn_done = sem("kn_ps"), sem("kn_done")
        sc_ps, sc_hi, sc_lo = sem("sc_ps"), sem("sc_hi"), sem("sc_lo")
        o_ps, den_add, den_rec, at_done = sem("o_ps"), sem("den_add"), sem("den_rec"), sem("at_done")
        u_ps, ut_done, state_new = sem("u_ps"), sem("ut_done"), sem("state_new")
        aT_ps, aT_hi, aT_lo, wo_ps = sem("aT_ps"), sem("aT_hi"), sem("aT_lo"), sem("wo_ps")
        x1_done, x1_out = sem("x1_done"), sem("x1_out")
        xn2_done, xn2T_ps, xn2T_done, lg_ps = sem("xn2_done"), sem("xn2T_ps"), sem("xn2T_done"), sem("lg_ps")
        rt = sem("rt")
        top_gap, top_exp = sem("top_gap"), sem("top_exp")
        cnt_done, carry_done, pos_ps = sem("cnt_done"), sem("carry_done"), sem("pos_ps")
        slot_done = sem("slot_done")
        scat_out = [sem("scat_out0"), sem("scat_out1")]
        tot_ps, tail_done, tail_out, tab = sem("tot_ps"), sem("tail_done"), sem("tail_out"), sem("tab")
        TAB = 20
        RT = 12

        def front_of(j, c):
            return 2 * j + c, j + c // 2

        LOOP0, LOOP1 = 5, 15
        END = STEPS + 3

        def iterations(engine, body):
            for c in range(LOOP0):
                body(0, c)
            with engine.Fori(0, (LOOP1 - LOOP0) // 2) as j:
                for c in (LOOP0, LOOP0 + 1):
                    body(j, c)
            for c in range(LOOP1, END):
                body(0, c)

        def real(j, c):
            return not isinstance(j, int) or 0 <= c < STEPS

        xg_in, y_out = [sem("xg_in0"), sem("xg_in1")], [sem("y_out0"), sem("y_out1")]
        w2_in = [sem("w2_in0"), sem("w2_in1")]
        b2_in, w2_hi, w2_lo = sem("b2_in"), sem("w2_hi"), sem("w2_lo")
        gt_ps, gt_hi, gt_lo, h_ps = sem("gt_ps"), sem("gt_hi"), sem("gt_lo"), sem("h_ps")
        gelu, g_hi, g_lo, y_ps, y_done = sem("gelu"), sem("g_hi"), sem("g_lo"), sem("y_ps"), sem("y_done")
        slot_copy, mix1, mixed = sem("slot_copy"), sem("mix1"), sem("mixed")
        ya_in, xo_in, out_out = [[sem(f"{n}{k}") for k in range(2)] for n in ("ya_in", "xo_in", "out_out")]
        W2Q = 4
        W2E = E // W2Q
        rows_T = [pR, pF[0]]
        hidden = [pS, [pO, pA]]
        y_bank = [pU, pF[1]]

        def tiles(engine, body, first=-2):
            for c in range(first, 2):
                body(0, c)
            with engine.Fori(0, (NT - 5) // 2) as j:
                for c in (2, 3):
                    body(j, c)
            for c in range(2 + (NT - 5) // 2 * 2, NT):
                body(0, c)

        def is_tile(j, c):
            return not isinstance(j, int) or 0 <= c < NT

        def last_steps(engine, body):
            for c in range(2):
                body(0, c)
            with engine.Fori(0, (STEPS - 2) // 2) as j:
                for c in (2, 3):
                    body(j, c)

        def carry_wait(engine):
            engine.sem_inc(passed[engine.engine], 1)

        block = ctx.enter_context(nc.Block())

        @block.sync
        def _(sp):
            sp.dma_start(cfs[:], cf).then_inc(consts_in, 16)
            sp.dma_start(chs[:], ch).then_inc(consts_in, 16)
            sp.dma_start(xs[:], x_steps[0]).then_inc(x_in, 16)
            sp.dma_start(bqks[:], bqk).then_inc(consts_in, 16)
            sp.dma_start(kst[:].bitcast(F32).rearrange("p a b c -> p (a b c)")[:, 0:4 * KC * D]
                         .rearrange("p (w n) -> p w n", w=4 * KC),
                         wqkvo.rearrange("w (k p) n -> p (w k) n", p=P)).then_inc(raw_in, 16)
            sp.dma_start(bvs[:], bv.partition_broadcast(P)).then_inc(consts_in, 16)
            sp.dma_start(bos[:], bo.partition_broadcast(P)).then_inc(consts_in, 16)
            sp.dma_start(rws[:], rw.rearrange("(k p) e -> p k e", p=P)).then_inc(consts_in, 16)
            sp.dma_start(b1s[:], b1).then_inc(consts_in, 16)
            qraw = qst[:].bitcast(F32).rearrange("p a b c d -> p (a b c d)")
            for hf in range(2):
                n = E * KC * F // 2
                sp.dma_start(qraw[:, hf * n:(hf + 1) * n], w1[:, hf * n:(hf + 1) * n]).then_inc(w1_in[hf], 16)
            sp.wait_ge(zero_set, 1)
            for n in range(E * MT // P):
                sp.dma_start(xg_dram[DUMMY + n * P:DUMMY + (n + 1) * P, :], zeros[:]).then_inc(pads_out, 16)

            def body(j, c):
                i, _ = front_of(j, c)
                s, sh = front_of(j, c - 1)
                if real(j, c + 1):
                    sp.wait_ge(xb_done, i + 1)
                    sp.dma_start(xs[:], x_steps[bass.ds(i + 1, 1)].rearrange("i p b d -> p (i b) d")).then_inc(x_in, 16)
                if real(j, c):
                    par = c % 2
                    sp.wait_ge(qk_hi, 4 * i + 4)
                    sp.wait_ge(qk_lo, 4 * i + 4)
                    if c >= 2:
                        sp.wait_ge(stack_in[par], 144 * (j + c // 2))
                    sp.dma_start(qk_dram[par].rearrange("h m p n -> p (h m) n"),
                                 qkhl[:].rearrange("p h m n -> p (h m) n")).then_inc(qk_out, 16)
                    sp.wait_ge(qk_out, 16 * i + 16)
                    if c >= 2:
                        sp.wait_ge(sc_ps, 16 * (i - 1))
                    else:
                        sp.wait_ge(wsplit_lo, 6)
                        sp.wait_ge(qst_zero, 2)
                    rows = qk_dram[par].rearrange("h (t k) p n -> h t (k p) n", t=2)
                    for part in range(3):
                        src = rows[part // 2, 1].rearrange("(a r) n -> r a n", r=2 * HD)
                        sp.dma_start(kst[2 * HD * part:2 * HD * (part + 1), par], src).then_inc(stack_in[par], 16)
                        src = rows[part % 2, 0].rearrange("(a e d) n -> e d a n", e=2, d=HD)
                        for e in range(2):
                            r0 = 2 * HD * part + HD * e
                            sp.dma_start(qst[r0:r0 + HD, par, :, e], src[e]).then_inc(stack_in[par], 16)
                if real(j, c - 1):
                    sp.wait_ge(x1_done, 4 * s + 4)
                    sp.dma_start(x1_steps[bass.ds(s, 1)].rearrange("i p b d -> p (i b) d"), x1[:]).then_inc(x1_out, 16)

            iterations(sp, body)

            sp.wait_ge(tab, TAB)
            sp.wait_ge(x1_out, 16 * STEPS)
            for n in range(2):
                sp.wait_ge(scat_out[n], 128 * STEPS // 2)
            for n in range(W2Q):
                if n >= 2:
                    sp.wait_ge(w2_lo, n - 1)
                sp.dma_start(w2raw[:, n % 2].rearrange("p e f d -> p (e f d)"),
                             w2[:, n * W2E * FC * D:(n + 1) * W2E * FC * D]).then_inc(w2_in[n % 2], 16)
                if n == 1:
                    sp.wait_ge(tail_out, 16 * 2 * E)
                    sp.wait_ge(pads_out, 16 * E * MT // P)
                    sp.dma_start(b2s[:].rearrange("p e d -> p (e d)"), b2.partition_broadcast(P)).then_inc(b2_in, 16)

            def load(j, c):
                t, th = front_of(j, c)
                if not is_tile(j, c):
                    return
                row = sp.value_load(table[0:1, 0, bass.ds(t, 1)], min_val=0, max_val=ROWS - MT)
                if c >= 2:
                    sp.wait_ge(gt_ps, t - 1)
                sp.dma_start(xg[:, c % 2], xg_dram[bass.ds(row, MT), :].rearrange("(s p) d -> p s d", p=P)).then_inc(xg_in[c % 2], 16)

            tiles(sp, load, 0)

            def x1_load(j, c):
                i, ih = front_of(j, c)
                if c >= 2:
                    sp.wait_ge(out_out[c % 2], 16 * ih)
                sp.dma_start(xo[:, c % 2], x1_steps[bass.ds(i, 1)].rearrange("i p b d -> p (i b) d")).then_inc(xo_in[c % 2], 16)

            last_steps(sp, x1_load)
            for n in range(2):
                sp.wait_ge(out_out[n], 16 * STEPS // 2)

        @block.tensor
        def _(pe):
            def split3(out, lhs, rhs, n, first=True):
                terms = [(a, b_, k) for a, b_ in ((0, 0), (0, 1), (1, 0)) for k in range(n)]
                for t, (a, b_, k) in enumerate(terms):
                    mm = nc.tensor.matmul(out, lhs(a, k), rhs(b_, k), start=(t == 0), stop=(t == len(terms) - 1))
                return mm

            def body(j, c):
                i, _ = front_of(j, c)
                s, _ = front_of(j, c - 1)
                r, _ = front_of(j, c - 2)
                fr, bk, ro = real(j, c), real(j, c - 1), real(j, c - 2)
                par, sp_ = c % 2, (c - 1) % 2
                first_s, first_r = c == 1, c == 2

                def x_transposes():
                    pe.wait_ge(xn_done, 4 * i + 4)
                    for k in range(KC):
                        if c >= 1:
                            pe.wait_ge(v_done, 2 * i - 1 + k)
                        for b in range(B):
                            mm = nc.tensor.transpose(pF[k][:, b * C:(b + 1) * C], xn[:, b, k * P:(k + 1) * P], ident)
                        mm.then_inc(xT_ps, 1)

                def project(m):
                    if m == 0:
                        pe.wait_ge(xT_lo, 2 * i + 2)
                        if c == 0:
                            pe.wait_ge(wsplit_lo, 4)
                    if m >= 2:
                        pe.wait_ge(qk_lin, 4 * i + m - 1)
                    w, k0 = m // 2, (m % 2) * P
                    split3(pF[m % 2][:], lambda a, k: was[:, a, w, k, k0:k0 + P], lambda a, k: xT[:, a, k], KC).then_inc(qk_ps, 1)

                def values(n):
                    pe.wait_ge(qk_lin, 4 * i + 3 + n)
                    for b in (2 * n, 2 * n + 1):
                        mm = split3(pF[n][:, (b % 2) * D:(b % 2 + 1) * D], lambda a, k: xT[:, a, k, b * C:(b + 1) * C],
                                    lambda a, k: was[:, a, 2, k], KC)
                    mm.then_inc(v_ps, 1)

                def k_rows(n):
                    if n == 0:
                        pe.wait_ge(qk_f, 4 * s + 4)
                        if not first_s:
                            pe.wait_ge(ut_done, 4 * s)
                    else:
                        pe.wait_ge(kn_done, 2 * s + 1)
                    for b in (2 * n, 2 * n + 1):
                        for k in range(KC):
                            c0 = (b % 2) * D + k * P
                            mm = nc.tensor.transpose(pU[:, c0:c0 + P], qk[:, sp_, 2 + k, b * C:(b + 1) * C], ident)
                    mm.then_inc(kn_ps, 1)

                def scores(b):
                    if b == 0:
                        pe.wait_ge(stack_in[sp_], 144 * (j + (c - 1) // 2 + 1))
                    for n in range(4):
                        g = 16 * s + 4 * b + n
                        if not (first_s and 4 * b + n < 2):
                            pe.wait_ge(sc_lo, g - 1)
                        o = pS[n % 2]
                        nc.tensor.matmul(o[:], ident16, mask16, start=True, stop=False, skip_group_check=True)
                        for e in range(2):
                            pr = 2 * n + e
                            mm = nc.tensor.matmul(o[:, e * 2 * C:(e + 1) * 2 * C], kst[0:STACK, sp_, pr, b * C:(b + 1) * C],
                                                  qst[0:STACK, sp_, pr, :, b * C:(b + 1) * C], start=False, stop=(e == 1),
                                                  skip_group_check=True)
                        mm.then_inc(sc_ps, 1)

                def attend(b):
                    g = 4 * s + b
                    if first_s:
                        pe.wait_ge(zero_set, 2)
                    else:
                        pe.wait_ge(state_new, 4 * s - 3 + b)
                    if not (first_s and b == 0):
                        pe.wait_ge(at_done, g)
                    for k in range(KC):
                        nc.tensor.matmul(pO[:, k * HC * VC:(k + 1) * HC * VC], qk[:, sp_, k, b * C:(b + 1) * C], state[:, b, k],
                                         start=(k == 0), stop=False, skip_group_check=True)
                    pe.wait_ge(sc_lo, 4 * g + 4)
                    pe.wait_ge(v_lo, s + 1)
                    for h in range(H):
                        for a, b_ in ((0, 0), (0, 1), (1, 0)):
                            mm = nc.tensor.matmul(pO[:, h * VC:(h + 1) * VC], ahl[:, b % 2, a, h * C:(h + 1) * C],
                                                  vhl[:, sp_, b_, b, h * VC:(h + 1) * VC], start=False,
                                                  stop=(h == H - 1 and a == 1), skip_group_check=True)
                    mm.then_inc(o_ps, 1)
                    pe.wait_ge(kn_done, 2 * s + 1 + (b >= 2))
                    if not (first_s and b == 0):
                        pe.wait_ge(ut_done, g)
                    if b < 2:
                        pe.wait_ge(kn_done, 2 * s + 2)
                    for k in range(KC):
                        mm = nc.tensor.matmul(pU[:, k * HC * VC:(k + 1) * HC * VC], kn[:, b, k * P:(k + 1) * P],
                                              v[:, sp_, b, k * HC:(k + 1) * HC].rearrange("p h c -> p (h c)"), start=True, stop=True)
                    mm.then_inc(u_ps, 1)

                def out_transpose(b):
                    g = 4 * s + b
                    pe.wait_ge(at_done, g + 1)
                    if not (first_s and b == 0):
                        pe.wait_ge(x1_done, g)
                    for k in range(KC):
                        mm = nc.tensor.transpose(pA[:, k * C:(k + 1) * C], at[:, k * P:(k + 1) * P], ident)
                    mm.then_inc(aT_ps, 1)

                def out_project(b):
                    g = 4 * s + b
                    pe.wait_ge(aT_lo, g + 1)
                    split3(pA[:, D:2 * D], lambda a, k: aT[:, a, k], lambda a, k: was[:, a, 3, k], KC).then_inc(wo_ps, 1)

                def route_transpose(b):
                    g = 4 * r + b
                    if b == 0:
                        pe.wait_ge(xn2_done, 4 * r + 4)
                        if not first_r:
                            pe.wait_ge(slot_done, r)
                    for k in range(KC):
                        mm = nc.tensor.transpose(pR[:, k * C:(k + 1) * C], xn2[:, c % 2, b, k * P:(k + 1) * P], ident)
                    mm.then_inc(xn2T_ps, 1)

                def route_logits(b):
                    g = 4 * r + b
                    pe.wait_ge(xn2T_done, g + 1)
                    for k in range(KC):
                        mm = nc.tensor.matmul(pR[:, LOGITS + b * E:LOGITS + (b + 1) * E], xn2T[:, k], rws[:, k],
                                              start=(k == 0), stop=(k == KC - 1))
                    mm.then_inc(lg_ps, 1)

                def route_positions():
                    pe.wait_ge(cnt_done, r + 1)
                    if not first_r:
                        pe.wait_ge(carry_done, r)
                    else:
                        pe.wait_ge(zero_set, 3)
                    o = pR[:, POS:POS + B * E]
                    nc.tensor.matmul(o, chs[:, H_TRI:H_TRI + P], cnt[:].rearrange("p b e -> p (b e)"), start=True, stop=False,
                                     skip_group_check=True)
                    for d in range(1, B):
                        nc.tensor.matmul(o[:, d * E:], chs[:, H_ONES:H_ONES + P],
                                         cnt[:, 0:B - d].rearrange("p b e -> p (b e)"), start=False, stop=False,
                                         skip_group_check=True)
                    nc.tensor.matmul(o, chs[:, H_ONES:H_ONES + P], carry[:].unsqueeze(1).to_broadcast([P, B, E]), start=False,
                                     stop=True, skip_group_check=True).then_inc(pos_ps, 1)

                if bk:
                    k_rows(0)
                    k_rows(1)
                    scores(0)
                if fr:
                    x_transposes()
                if bk:
                    scores(1)
                if fr:
                    project(0)
                    project(1)
                if ro:
                    route_transpose(0)
                if bk:
                    attend(0)
                if ro:
                    route_logits(0)
                if bk:
                    scores(2)
                if fr:
                    project(2)
                    project(3)
                if ro:
                    route_transpose(1)
                if bk:
                    out_transpose(0)
                    attend(1)
                    out_project(0)
                if ro:
                    route_logits(1)
                if bk:
                    scores(3)
                if ro:
                    route_transpose(2)
                if fr:
                    values(0)
                    values(1)
                if bk:
                    out_transpose(1)
                    attend(2)
                if ro:
                    route_logits(2)
                if bk:
                    out_project(1)
                if ro:
                    route_transpose(3)
                if bk:
                    out_transpose(2)
                    attend(3)
                if ro:
                    route_logits(3)
                if bk:
                    out_project(2)
                    out_transpose(3)
                if ro:
                    route_positions()
                if bk:
                    out_project(3)

            pe.wait_ge(consts_in, CONSTS)
            iterations(pe, body)
            pe.wait_ge(carry_done, STEPS)
            pe.wait_ge(slot_done, STEPS)
            nc.tensor.matmul(pR[:, 0:E], chs[:, H_ONES:H_ONES + P], carry[:], start=True, stop=True).then_inc(tot_ps, 1)

            def tile(j, c):
                t, th = front_of(j, c)

                def hidden_layer():
                    p1 = (c + 1) % 2
                    e = pe.value_load(table[0:1, 1, bass.ds(t + 1, 1)], min_val=0, max_val=E - 1)
                    pe.wait_ge(gt_lo, t + 2)
                    if c + 1 >= 2:
                        pe.wait_ge(gelu, 4 * t)
                    for f in range(FC):
                        mm = split3(hidden[p1][f // 2][:, (f % 2) * MT:(f % 2 + 1) * MT],
                                    lambda a, k: w1s[:, a, bass.ds(e, 1), k, f * P:(f + 1) * P].rearrange("p e f -> p (e f)"),
                                    lambda a, k: gT[:, p1, a, k * MT:(k + 1) * MT], KC)
                        if f % 2:
                            mm.then_inc(h_ps, 1)

                def turn():
                    pe.wait_ge(xg_in[c % 2], 16 * (j + (c + 2) // 2 + 1))
                    if c + 2 >= 2:
                        pe.wait_ge(gt_lo, t + 1)
                    for k in range(KC):
                        for s in range(MT // P):
                            mm = nc.tensor.transpose(rows_T[c % 2][:, k * MT + s * P:k * MT + (s + 1) * P],
                                                     xg[:, c % 2, s, k * P:(k + 1) * P], ident)
                    mm.then_inc(gt_ps, 1)

                def second_layer():
                    e = pe.value_load(table[0:1, 1, bass.ds(t, 1)], min_val=0, max_val=E - 1)
                    pe.wait_ge(g_lo, t + 1)
                    if c == 0:
                        pe.wait_ge(w2_lo, W2Q)
                    if c >= 2:
                        pe.wait_ge(y_done, t - 1)
                    for s in range(MT // P):
                        mm = split3(y_bank[c % 2][:, s * D:(s + 1) * D], lambda a, f: ghl[:, c % 2, a, f, s * P:(s + 1) * P],
                                    lambda a, f: w2s[:, a, bass.ds(e, 1), f].rearrange("p e d -> p (e d)"), FC)
                    mm.then_inc(y_ps, 1)

                if is_tile(j, c + 1):
                    hidden_layer()
                if is_tile(j, c + 2):
                    turn()
                if is_tile(j, c):
                    second_layer()

            pe.wait_ge(tab, TAB)
            tiles(pe, tile)

        @block.scalar
        def _(act):
            act.dma_start(cbs[:], cb).then_inc(consts_in, 16)
            act.wait_ge(raw_in, 16)
            raw = kst[:].bitcast(F32).rearrange("p a b c -> p (a b c)")[:, 0:4 * KC * D].rearrange("p (w k n) -> p w k n", w=4, k=KC)
            for w in range(4):
                nc.scalar.activation(was[:, 0, w], raw[:, w], ACT.Copy, scale=WS).then_inc(wsplit_hi, 1)
            qraw = qst[:].bitcast(F32).rearrange("p a b c d -> p (a b c d)").rearrange("p (e k f) -> p e k f", e=E, k=KC)
            act.wait_ge(consts_in, CONSTS)

            def body(j, c):
                i, _ = front_of(j, c)
                s, _ = front_of(j, c - 1)
                r, _ = front_of(j, c - 2)
                fr, bk, ro = real(j, c), real(j, c - 1), real(j, c - 2)
                par = c % 2

                def kn_rows(n):
                    act.wait_ge(kn_ps, 2 * s + 1 + n)
                    if c >= 2:
                        act.wait_ge(u_ps, 4 * s)
                    nc.scalar.activation(kn[:, 2 * n:2 * n + 2].rearrange("p b d -> p (b d)"), pU[:], ACT.Copy).then_inc(kn_done, 1)

                def score_hi(b):
                    for n in range(4):
                        g = 16 * s + 4 * b + n
                        act.wait_ge(sc_ps, g + 1)
                        if n == 0 and not (c == 1 and b < 2):
                            act.wait_ge(o_ps, 4 * s + b - 1)
                        nc.scalar.activation(ahl[:, b % 2, 0, n * 4 * C:(n + 1) * 4 * C], pS[n % 2][:], ACT.Relu).then_inc(sc_hi, 1)

                def x_hi():
                    for k in range(KC):
                        act.wait_ge(xT_ps, 2 * i + k + 1)
                        if c >= 1:
                            act.wait_ge(v_ps, 2 * i)
                        nc.scalar.activation(xT[:, 0, k], pF[k][:], ACT.Copy).then_inc(xT_hi, 1)

                def feature(m):
                    act.wait_ge(qk_ps, 4 * i + m + 1)
                    if not (c == 0 and m < 2):
                        act.wait_ge(qk_f, 4 * i + m - 1)
                    e_, l_ = et[:, m % 2], lt[:, m % 2]
                    nc.scalar.activation(e_, pF[m % 2][:], ACT.Relu, bias=negb[:, m:m + 1], scale=-1.0 / WS).then_inc(qk_neg, 1)
                    nc.scalar.activation(l_, pF[m % 2][:], ACT.Relu, bias=linb[:, m:m + 1], scale=QS / WS).then_inc(qk_lin, 1)
                    act.wait_ge(qk_neg, 8 * i + 2 * m + 1)
                    nc.scalar.activation(e_, e_, ACT.Exp, bias=cfs[:, C_LN:C_LN + 1], scale=-1.0).then_inc(qk_neg, 1)

                def qk_high(m):
                    act.wait_ge(qk_f, 4 * i + m + 1)
                    if c >= 1:
                        act.wait_ge(qk_out, 16 * i)
                    nc.scalar.activation(qkhl[:, 0, m], qk[:, par, m], ACT.Copy).then_inc(qk_hi, 1)

                def v_high():
                    act.wait_ge(v_done, 2 * i + 2)
                    if c >= 2:
                        act.wait_ge(o_ps, 4 * (i - 1))
                    nc.scalar.activation(vhl[:, par, 0].rearrange("p b n -> p (b n)"),
                                         v[:, par].rearrange("p b h c -> p (b h c)"), ACT.Copy).then_inc(v_hi, 1)

                def row_copy(b):
                    g = 4 * r + b
                    act.wait_ge(xn2T_ps, g + 1)
                    if not (c == 2 and b == 0):
                        act.wait_ge(lg_ps, g)
                    nc.scalar.activation(xn2T[:].rearrange("p k n -> p (k n)"), pR[:, 0:KC * C], ACT.Copy).then_inc(xn2T_done, 1)

                def out_hi(b):
                    g = 4 * s + b
                    act.wait_ge(aT_ps, g + 1)
                    nc.scalar.activation(aT[:, 0].rearrange("p k n -> p (k n)"), pA[:, 0:KC * C], ACT.Copy).then_inc(aT_hi, 1)

                if bk:
                    kn_rows(0)
                    kn_rows(1)
                    score_hi(0)
                if fr:
                    x_hi()
                if bk:
                    score_hi(1)
                if fr:
                    feature(0)
                    feature(1)
                if ro:
                    row_copy(0)
                if bk:
                    score_hi(2)
                if fr:
                    qk_high(0)
                    feature(2)
                    qk_high(1)
                    feature(3)
                if ro:
                    row_copy(1)
                if bk:
                    out_hi(0)
                    score_hi(3)
                if ro:
                    row_copy(2)
                if fr:
                    qk_high(2)
                    qk_high(3)
                if bk:
                    out_hi(1)
                if ro:
                    row_copy(3)
                if bk:
                    out_hi(2)
                if fr:
                    v_high()
                if bk:
                    out_hi(3)
                if ro:
                    act.wait_ge(top_gap, r + 1)
                    nc.scalar.activation(pd[:, 1], pd[:, 0], ACT.Exp).then_inc(top_exp, 1)
                if c == 0:
                    for hf in range(2):
                        act.wait_ge(w1_in[hf], 16)
                        e0 = hf * E // 2
                        nc.scalar.activation(w1s[:, 0, e0:e0 + E // 2].rearrange("p e k f -> p (e k f)"),
                                             qraw[:, e0:e0 + E // 2].rearrange("p e k f -> p (e k f)"), ACT.Copy,
                                             scale=WS).then_inc(wsplit_hi, 1)

            iterations(act, body)
            for n in range(W2Q):
                act.wait_ge(w2_in[n % 2], 16 * (n // 2 + 1))
                nc.scalar.activation(w2s[:, 0, n * W2E:(n + 1) * W2E].rearrange("p e f d -> p (e f d)"),
                                     w2raw[:, n % 2].rearrange("p e f d -> p (e f d)"), ACT.Copy, scale=WS).then_inc(w2_hi, 1)

            def tile(j, c):
                t, _ = front_of(j, c)
                if is_tile(j, c + 1):
                    p1 = (c + 1) % 2
                    e = act.value_load(table[0:1, 1, bass.ds(t + 1, 1)], min_val=0, max_val=E - 1)
                    if c + 1 >= 2:
                        act.wait_ge(g_lo, t)
                    for f in range(FC):
                        act.wait_ge(h_ps, 2 * t + 3 + f // 2)
                        nc.scalar.activation(g[:, p1, f], hidden[p1][f // 2][:, (f % 2) * MT:(f % 2 + 1) * MT], ACT.Gelu,
                                             bias=b1s[:, bass.ds(e * FC + f, 1)], scale=1.0 / WS).then_inc(gelu, 1)
                if is_tile(j, c + 2):
                    act.wait_ge(gt_ps, t + 3)
                    if c + 2 >= 2:
                        act.wait_ge(h_ps, 2 * t + 2)
                    nc.scalar.activation(gT[:, c % 2, 0], rows_T[c % 2][:], ACT.Copy).then_inc(gt_hi, 1)

            act.wait_ge(tab, TAB)
            tiles(act, tile)

            def store(j, c):
                i, _ = front_of(j, c)
                act.wait_ge(mixed, 4 * i + 4)
                act.dma_start(out_steps[bass.ds(i, 1)].rearrange("i p b d -> p (i b) d"), xo[:, c % 2]).then_inc(out_out[c % 2], 16)

            last_steps(act, store)

        @block.vector
        def _(dve):
            V = nc.vector
            V.memset(zeros[:], 0.0).then_inc(zero_set, 1)
            V.memset(state[:].rearrange("p a b c -> p (a b c)"), 0.0).then_inc(zero_set, 1)
            V.memset(carry[:], 0.0).then_inc(zero_set, 1)
            for par in range(2):
                V.memset(v[:, par].rearrange("p b h c -> p (b h) c")[:, :, HD:VC], 1.0).then_inc(ones_set, 1)
            dve.wait_ge(consts_in, CONSTS)
            V.tensor_scalar(negb[:], bqks[:], -1.0, None, ALU.mult).then_inc(bias_prep, 1)
            V.tensor_scalar(linb[:], bqks[:], QS, None, ALU.mult).then_inc(bias_prep, 1)
            raw = kst[:].bitcast(F32).rearrange("p a b c -> p (a b c)")[:, 0:4 * KC * D].rearrange("p (w k n) -> p w k n", w=4, k=KC)
            qraw = qst[:].bitcast(F32).rearrange("p a b c d -> p (a b c d)").rearrange("p (e k f) -> p e k f", e=E, k=KC)

            def norm_stats(i, c, src, st, mv, ve, sems, ready):
                ready()
                for b in range(B):
                    V.bn_stats(st[:, b], src[:, b]).then_inc(sems[0], 1)
                dve.wait_ge(sems[0], 4 * i + 4)
                carry_wait(dve)
                for b in range(B):
                    V.bn_aggr(mv[:, b], st[:, b]).then_inc(sems[1], 1)
                dve.wait_ge(sems[1], 4 * i + 4)
                V.tensor_scalar(ve[:], mv[:, :, 1], EPS, None, ALU.add).then_inc(sems[2], 1)

            def norm1_stats(i, c):
                norm_stats(i, c, xs, st1, mv1, ve1, (ln1_st, ln1_mv, ln1_ve), lambda: dve.wait_ge(x_in, 16 * i + 16))

            def norm1_apply(i, c):
                dve.wait_ge(ln1_rs, i + 1)
                if c >= 1:
                    dve.wait_ge(xT_ps, 2 * i)
                for b in range(B):
                    V.tensor_scalar(xn[:, b], xs[:, b], mv1[:, b, 0:1], rs1[:, b:b + 1], ALU.subtract, ALU.mult).then_inc(xn_done, 1)

            def body(j, c):
                i, _ = front_of(j, c)
                s, _ = front_of(j, c - 1)
                r, rh = front_of(j, c - 2)
                fr, bk, ro, nx = real(j, c), real(j, c - 1), real(j, c - 2), real(j, c + 1)
                par, sp_, rp = c % 2, (c - 1) % 2, c % 2

                def score_lo(b):
                    for n in range(4):
                        g = 16 * s + 4 * b + n
                        dve.wait_ge(sc_hi, g + 1)
                        cols = slice(n * 4 * C, (n + 1) * 4 * C)
                        V.scalar_tensor_tensor(ahl[:, b % 2, 1, cols], pS[n % 2][:], 0.0, ahl[:, b % 2, 0, cols], ALU.max,
                                               ALU.subtract).then_inc(sc_lo, 1)

                def x_lo():
                    for k in range(KC):
                        dve.wait_ge(xT_hi, 2 * i + k + 1)
                        V.tensor_tensor(xT[:, 1, k], pF[k][:], xT[:, 0, k], ALU.subtract).then_inc(xT_lo, 1)

                def norm2_apply():
                    dve.wait_ge(ln2_rs, r + 1)
                    if c >= 4:
                        dve.wait_ge(scat_out[rp], 128 * rh)
                    for b in range(B):
                        V.tensor_scalar(xn2[:, rp, b], x1[:, b], mv2[:, b, 0:1], rs2[:, b:b + 1], ALU.subtract, ALU.mult).then_inc(xn2_done, 1)

                def attention(b):
                    g = 4 * s + b
                    dve.wait_ge(o_ps, g + 1)
                    o = pO[:, 0:H * VC].rearrange("p (h c) -> p h c", c=VC)
                    V.tensor_scalar(rden[:, 0], o[:, :, HD], DEN_EPS, None, ALU.add).then_inc(den_add, 1)
                    dve.wait_ge(den_add, g + 1)
                    V.reciprocal(rden[:, 1], rden[:, 0]).then_inc(den_rec, 1)
                    dve.wait_ge(den_rec, g + 1)
                    if not (c == 1 and b == 0):
                        dve.wait_ge(aT_ps, g)
                    V.tensor_tensor(at[:].rearrange("p (h c) -> p h c", c=HD), o[:, :, 0:HD],
                                    rden[:, 1].unsqueeze(2).to_broadcast([P, H, HD]), ALU.mult).then_inc(at_done, 1)

                def state_part(b):
                    g = 4 * s + b
                    dve.wait_ge(u_ps, g + 1)
                    if not (c == 1 and b == 0):
                        dve.wait_ge(state_new, g)
                    V.tensor_tensor(ut[:], pU[:, 0:KC * HC * VC], block_mask, ALU.mult).then_inc(ut_done, 1)

                def out_lo(b):
                    g = 4 * s + b
                    dve.wait_ge(aT_hi, g + 1)
                    V.tensor_tensor(aT[:, 1].rearrange("p k n -> p (k n)"), pA[:, 0:KC * C], aT[:, 0].rearrange("p k n -> p (k n)"),
                                    ALU.subtract).then_inc(aT_lo, 1)

                def residual(b):
                    g = 4 * s + b
                    dve.wait_ge(wo_ps, g + 1)
                    if b == 0:
                        dve.wait_ge(xb_done, s + 1)
                        if c >= 2:
                            dve.wait_ge(x1_out, 16 * s)
                            dve.wait_ge(xn2_done, 4 * s)
                    V.scalar_tensor_tensor(x1[:, b], pA[:, D:2 * D], 1.0 / WS, xb[:, sp_, b], ALU.mult, ALU.add).then_inc(x1_done, 1)

                def values(n):
                    dve.wait_ge(v_ps, 2 * i + 1 + n)
                    if c >= 2 and n == 0:
                        dve.wait_ge(u_ps, 4 * (i - 1))
                    V.scalar_tensor_tensor(v[:, par, 2 * n:2 * n + 2, :, 0:HD],
                                           pF[n][:].rearrange("p (b h c) -> p b h c", b=2, h=H), 1.0 / WS,
                                           bvs[:].rearrange("p (h c) -> p h c", h=H).unsqueeze(1).to_broadcast([P, 2, H, HD]),
                                           ALU.mult, ALU.add).then_inc(v_done, 1)

                links = [0]

                def link(ins):
                    links[0] += 1
                    ins.then_inc(rt, 1)
                    dve.wait_ge(rt, RT * r + links[0])

                def router():
                    dve.wait_ge(lg_ps, 4 * r + 4)
                    link(V.tensor_copy(lg[:].rearrange("p b e -> p (b e)"), pR[:, LOGITS:LOGITS + B * E]))
                    carry_wait(dve)
                    for b in range(B):
                        ins = V.max(mx[:, b], lg[:, b])
                    link(ins)
                    carry_wait(dve)
                    for b in range(B):
                        ins = V.max_index(ix[:, b], mx[:, b], lg[:, b])
                    V.tensor_tensor(pd[:, 0], mx[:, :, 1], mx[:, :, 0], ALU.subtract).then_inc(top_gap, 1)
                    link(ins)
                    link(V.tensor_copy(ixf[:], ix[:, :, 0:2]))
                    link(V.tensor_tensor(oh[:].rearrange("p b t e -> p (b t) e"),
                                         cfs[:, C_IOTA8:C_IOTA8 + E].unsqueeze(1).to_broadcast([P, 2 * B, E]),
                                         ixf[:].rearrange("p b t -> p (b t)").unsqueeze(2).to_broadcast([P, 2 * B, E]), ALU.is_equal))
                    V.tensor_tensor(cnt[:], oh[:, :, 0], oh[:, :, 1], ALU.add).then_inc(cnt_done, 1)

                def router_probs():
                    dve.wait_ge(top_exp, r + 1)
                    p1, p2 = probs[:, bass.ds(r, 1), 0], probs[:, bass.ds(r, 1), 1]
                    link(V.tensor_scalar(pd[:, 0], pd[:, 1], 1.0, None, ALU.add))
                    link(V.reciprocal(pd[:, 0], pd[:, 0]))
                    V.tensor_copy(p1.rearrange("p i b -> p (i b)"), pd[:, 0])
                    link(V.tensor_tensor(p2.rearrange("p i b -> p (i b)"), pd[:, 0], pd[:, 1], ALU.mult))

                def router_slots():
                    dve.wait_ge(pos_ps, r + 1)
                    caps = cfs[:, C_CAPS:C_CAPS + E].unsqueeze(1).to_broadcast([P, B, E])
                    link(V.tensor_tensor(pos[:], pR[:, POS:POS + B * E].rearrange("p (b e) -> p b e", b=B), caps, ALU.add))
                    link(V.tensor_tensor(sel[:], oh[:], pos[:].unsqueeze(2).to_broadcast([P, B, 2, E]), ALU.mult))
                    link(V.tensor_reduce(slf[:], sel[:].rearrange("p b t e -> p (b t) e"), AX.X, ALU.add))
                    if c >= 4:
                        dve.wait_ge(scat_out[rp], 128 * rh)
                    V.tensor_copy(slots[:, bass.ds(r, 1)].rearrange("p i n -> p (i n)"), slf[:])
                    V.tensor_copy(cur[:, rp], slf[:]).then_inc(slot_done, 1)
                    with nc.allow_low_precision("counts up to 128 are exact in float16"):
                        V.tensor_reduce(ctmp[:], cnt[:].rearrange("p b e -> p e b"), AX.X, ALU.add).then_inc(rt, 1)
                        links[0] += 1
                        dve.wait_ge(rt, RT * r + links[0])
                        V.tensor_tensor(carry[:], carry[:], ctmp[:], ALU.add).then_inc(carry_done, 1)
                    assert links[0] == RT, links

                if ro:
                    norm_stats(r, c, x1, st2, mv2, ve2, (ln2_st, ln2_mv, ln2_ve), lambda: dve.wait_ge(x1_done, 4 * r + 4))
                if bk:
                    score_lo(0)
                if fr:
                    x_lo()
                if ro:
                    norm2_apply()
                if bk:
                    score_lo(1)
                if bk:
                    attention(0)
                    state_part(0)
                if nx:
                    norm1_stats(i + 1, c + 1)
                if bk:
                    score_lo(2)
                    out_lo(0)
                    attention(1)
                    state_part(1)
                    residual(0)
                    score_lo(3)
                if fr:
                    values(0)
                    values(1)
                if bk:
                    out_lo(1)
                    attention(2)
                    state_part(2)
                    residual(1)
                if nx:
                    norm1_apply(i + 1, c + 1)
                if bk:
                    out_lo(2)
                    attention(3)
                    state_part(3)
                if ro:
                    router()
                if bk:
                    residual(2)
                if ro:
                    router_probs()
                if bk:
                    out_lo(3)
                if ro:
                    router_slots()
                if bk:
                    residual(3)
                if c == 0:
                    for hf in range(2):
                        dve.wait_ge(wsplit_hi, 5 + hf)
                        e0 = hf * E // 2
                        V.scalar_tensor_tensor(w1s[:, 1, e0:e0 + E // 2].rearrange("p e k f -> p (e k f)"),
                                               qraw[:, e0:e0 + E // 2].rearrange("p e k f -> p (e k f)"), WS,
                                               w1s[:, 0, e0:e0 + E // 2].rearrange("p e k f -> p (e k f)"), ALU.mult,
                                               ALU.subtract).then_inc(wsplit_lo, 1)
                    dve.wait_ge(wsplit_lo, 6)
                    for hf in range(2):
                        V.memset(qst[:, hf].bitcast(F32).rearrange("p a b c -> p (a b c)"), 0.0).then_inc(qst_zero, 1)

            dve.wait_ge(wsplit_hi, 4)
            for w in range(4):
                V.scalar_tensor_tensor(was[:, 1, w], raw[:, w], WS, was[:, 0, w], ALU.mult, ALU.subtract).then_inc(wsplit_lo, 1)
            norm1_stats(0, 0)
            norm1_apply(0, 0)
            iterations(dve, body)

            done = [0]

            def chain(ins):
                done[0] += 1
                ins.then_inc(tab, 1)
                dve.wait_ge(tab, done[0])

            dve.wait_ge(tot_ps, 1)
            caps = cfs[:, C_CAPS:C_CAPS + E]
            chain(V.tensor_copy(tiles_f[:, 0], pR[:, 0:E]))
            for n in range(2):
                ins = V.tensor_tensor(tails[:, n], tiles_f[:, 0], caps, ALU.add)
            chain(ins)
            for n in range(2):
                V.tensor_scalar(tails_i[:, n], tails[:, n], cfs[:, C_ROW0 + n:C_ROW0 + n + 1], None, ALU.add).then_inc(tail_done, 1)
            chain(V.tensor_scalar(tiles_i[:], tiles_f[:, 0], float(MT - 1), None, ALU.add))
            chain(V.tensor_scalar(tiles_i[:], tiles_i[:], int(math.log2(MT)), None, ALU.logical_shift_right))
            chain(V.tensor_copy(tiles_f[:, 1], tiles_i[:]))
            mine = tiles_f[0:1, 1]
            chain(V.tensor_tensor(upto, mine.unsqueeze(1).to_broadcast([1, E, E]),
                                  cfs[0:1, C_TRI8:C_TRI8 + E * E].rearrange("p (a b) -> p a b", a=E), ALU.mult))
            chain(V.tensor_reduce(tiles_f[0:1, 2], upto, AX.X, ALU.add))
            number = cfs[0:1, C_TILES:C_TILES + NT]
            chain(V.tensor_tensor(past, number.unsqueeze(2).to_broadcast([1, NT, E]),
                                  tiles_f[0:1, 2].unsqueeze(1).to_broadcast([1, NT, E]), ALU.is_ge))
            chain(V.tensor_reduce(tj[:, 0], past, AX.X, ALU.add))
            chain(V.tensor_tensor(past_tiles, past, mine.unsqueeze(1).to_broadcast([1, NT, E]), ALU.mult))
            chain(V.tensor_reduce(tj[:, 1], past_tiles, AX.X, ALU.add))
            chain(V.tensor_tensor(tj[:, 2], number, tj[:, 1], ALU.subtract))
            chain(V.tensor_scalar(tj[:, 3], tj[:, 0], float(CAP), None, ALU.mult))
            chain(V.scalar_tensor_tensor(table[:, 0], tj[:, 2], float(MT), tj[:, 3], ALU.mult, ALU.add))
            chain(V.tensor_scalar(table[:, 1], tj[:, 0], float(E - 1), None, ALU.min))
            chain(V.tensor_scalar(tiles_f[:, 3], tiles_f[:, 1], float(MT), float(-CAP), ALU.mult, ALU.add))
            every = slots[:].rearrange("p i n -> p (i n)")
            chain(V.tensor_tensor(behind, every.unsqueeze(2).to_broadcast([P, STEPS * 2 * B, E - 1]),
                                  caps[:, 1:E].unsqueeze(1).to_broadcast([P, STEPS * 2 * B, E - 1]), ALU.is_ge))
            chain(V.tensor_tensor(shift, behind, tiles_f[:, 3, 0:E - 1].unsqueeze(1).to_broadcast([P, STEPS * 2 * B, E - 1]),
                                  ALU.mult))
            moved = behind.rearrange("p s e -> p (s e)")[:, 0:STEPS * 2 * B]
            chain(V.tensor_reduce(moved, shift, AX.X, ALU.add))
            chain(V.tensor_tensor(y_slots[:].rearrange("p i n -> p (i n)"), every, moved, ALU.add))
            assert done[0] == TAB, done

            for n in range(W2Q):
                dve.wait_ge(w2_hi, n + 1)
                lot = lambda x: x.rearrange("p e f d -> p (e f d)")
                V.scalar_tensor_tensor(lot(w2s[:, 1, n * W2E:(n + 1) * W2E]), lot(w2raw[:, n % 2]), WS,
                                       lot(w2s[:, 0, n * W2E:(n + 1) * W2E]), ALU.mult, ALU.subtract).then_inc(w2_lo, 1)

            def tile(j, c):
                t, th = front_of(j, c)
                if is_tile(j, c + 1):
                    p1 = (c + 1) % 2
                    dve.wait_ge(gelu, 4 * t + 8)
                    if c + 1 >= 2:
                        dve.wait_ge(y_ps, t)
                    V.tensor_copy(ghl[:, p1, 0].rearrange("p f n -> p (f n)"), g[:, p1].rearrange("p f n -> p (f n)")).then_inc(g_hi, 1)
                if is_tile(j, c + 2):
                    dve.wait_ge(gt_hi, t + 3)
                    V.tensor_tensor(gT[:, c % 2, 1], rows_T[c % 2][:], gT[:, c % 2, 0], ALU.subtract).then_inc(gt_lo, 1)
                if is_tile(j, c):
                    e = dve.value_load(table[0:1, 1, bass.ds(t, 1)], min_val=0, max_val=E - 1)
                    dve.wait_ge(y_ps, t + 1)
                    if c == 0:
                        dve.wait_ge(b2_in, 16)
                    if c >= 2:
                        dve.wait_ge(y_out[c % 2], 16 * th)
                    V.scalar_tensor_tensor(yt[:, c % 2], y_bank[c % 2][:].rearrange("p (s d) -> p s d", s=2), 1.0 / WS,
                                           b2s[:, bass.ds(e, 1)].to_broadcast([P, 2, D]), ALU.mult, ALU.add).then_inc(y_done, 1)

            tiles(dve, tile)

            def mix(j, c):
                i, ih = front_of(j, c)
                dve.wait_ge(xo_in[c % 2], 16 * ih + 16)
                dve.wait_ge(ya_in[c % 2], 128 * ih + 128)
                for t, done_ in ((0, mix1), (1, mixed)):
                    if t:
                        dve.wait_ge(mix1, 4 * i + 4)
                    for b in range(B):
                        weight = probs[:, bass.ds(i, 1), t, b:b + 1].rearrange("p i b -> p (i b)")
                        V.scalar_tensor_tensor(xo[:, c % 2, b], ya[:, c % 2, 2 * b + t], weight, xo[:, c % 2, b], ALU.mult,
                                               ALU.add).then_inc(done_, 1)

            last_steps(dve, mix)

        @block.gpsimd
        def _(pool):
            G = nc.gpsimd
            pool.wait_ge(consts_in, CONSTS)

            def rstd(i, ve, rs, made, done):
                pool.wait_ge(made, i + 1)
                G.tensor_tensor(rs[:], ve[:], cfs[:, C_POW:C_POW + B], ALU.pow).then_inc(done, 1)

            def add_bo(i, c):
                pool.wait_ge(xn_done, 4 * i + 4)
                if c >= 2:
                    pool.wait_ge(x1_done, 4 * (i - 1))
                G.tensor_tensor(xb[:, c % 2], xs[:], bos[:].unsqueeze(1).to_broadcast([P, B, D]), ALU.add).then_inc(xb_done, 1)

            def body(j, c):
                i, _ = front_of(j, c)
                s, _ = front_of(j, c - 1)
                r, _ = front_of(j, c - 2)
                q, qh = front_of(j, c - 3)
                fr, bk, ro, nx, sc = real(j, c), real(j, c - 1), real(j, c - 2), real(j, c + 1), real(j, c - 3)
                par, sp_, qp = c % 2, (c - 1) % 2, (c - 3) % 2

                def feature(m):
                    pool.wait_ge(qk_neg, 8 * i + 2 * m + 2)
                    pool.wait_ge(qk_lin, 4 * i + m + 1)
                    if c >= 2 and m == 0:
                        pool.wait_ge(o_ps, 4 * (i - 1))
                    G.tensor_tensor(qk[:, par, m], et[:, m % 2], lt[:, m % 2], ALU.add).then_inc(qk_f, 1)

                def low(m):
                    pool.wait_ge(qk_hi, 4 * i + m + 1)
                    G.tensor_tensor(qkhl[:, 1, m], qk[:, par, m], qkhl[:, 0, m], ALU.subtract).then_inc(qk_lo, 1)

                def state_add(b):
                    g = 4 * s + b
                    pool.wait_ge(ut_done, g + 1)
                    pool.wait_ge(o_ps, g + 1)
                    sb_ = state[:, b].rearrange("p k n -> p (k n)")
                    G.tensor_tensor(sb_, sb_, ut[:], ALU.add).then_inc(state_new, 1)

                if ro:
                    rstd(r, ve2, rs2, ln2_ve, ln2_rs)
                if sc:
                    pool.wait_ge(slot_done, q + 1)
                    carry_wait(pool)
                    for b in range(B):
                        for t in range(2):
                            G.indirect_dma_start(xg_dram, bass.IndirectOffsetOnAxis(ap=cur[:, qp, 2 * b + t:2 * b + t + 1], axis=0),
                                                 xn2[:, qp, b], None).then_inc(scat_out[qp], 16)
                if fr:
                    feature(0)
                    feature(1)
                if bk:
                    state_add(0)
                if nx:
                    rstd(i + 1, ve1, rs1, ln1_ve, ln1_rs)
                if fr:
                    low(0)
                    feature(2)
                    low(1)
                    feature(3)
                if bk:
                    state_add(1)
                if fr:
                    low(2)
                    low(3)
                if bk:
                    state_add(2)
                if nx:
                    add_bo(i + 1, c + 1)
                if fr:
                    pool.wait_ge(v_hi, i + 1)
                    G.tensor_tensor(vhl[:, par, 1].rearrange("p b n -> p (b n)"), v[:, par].rearrange("p b h c -> p (b h c)"),
                                    vhl[:, par, 0].rearrange("p b n -> p (b n)"), ALU.subtract).then_inc(v_lo, 1)
                if bk:
                    state_add(3)

            rstd(0, ve1, rs1, ln1_ve, ln1_rs)
            add_bo(0, 0)
            iterations(pool, body)
            pool.wait_ge(tail_done, 2)
            for e in range(E):
                for n in range(2):
                    G.indirect_dma_start(xg_dram, bass.IndirectOffsetOnAxis(ap=tails_i[:, n, e:e + 1], axis=0), zeros[:],
                                         None).then_inc(tail_out, 16)

            def tile(j, c):
                t, _ = front_of(j, c)
                if is_tile(j, c + 1):
                    p1 = (c + 1) % 2
                    pool.wait_ge(g_hi, t + 2)
                    G.tensor_tensor(ghl[:, p1, 1].rearrange("p f n -> p (f n)"), g[:, p1].rearrange("p f n -> p (f n)"),
                                    ghl[:, p1, 0].rearrange("p f n -> p (f n)"), ALU.subtract).then_inc(g_lo, 1)
                if is_tile(j, c):
                    pool.wait_ge(y_done, t + 1)
                    pool.dma_start(y_dram[bass.ds(t * MT, MT), :].rearrange("(s p) d -> p s d", p=P), yt[:, c % 2]).then_inc(y_out[c % 2], 16)

            pool.wait_ge(tab, TAB)
            tiles(pool, tile)
            for n in range(2):
                pool.wait_ge(y_out[n], 16 * ((NT + 1 - n) // 2))

            def gather(j, c):
                i, _ = front_of(j, c)
                if c >= 2:
                    pool.wait_ge(mixed, 4 * (i - 1))
                G.tensor_copy(curg[:, c % 2], y_slots[:, bass.ds(i, 1)].rearrange("p i n -> p (i n)")).then_inc(slot_copy, 1)
                pool.wait_ge(slot_copy, i + 1)
                carry_wait(pool)
                for n in range(2 * B):
                    G.indirect_dma_start(ya[:, c % 2, n], None, y_dram,
                                         bass.IndirectOffsetOnAxis(ap=curg[:, c % 2, n:n + 1], axis=0)).then_inc(ya_in[c % 2], 16)

            last_steps(pool, gather)


def kernel(**inputs):
    import numpy as np
    import concourse.bacc as bacc
    from concourse.bass_utils import run_bass_kernel_spmd

    a = {k.split("_", 2)[2]: np.asarray(val) for k, val in inputs.items()}
    f, h, b = constants()
    data = {
        "x": a["x"].reshape(T, D),
        "wqkvo": np.stack([a["Wq"], a["Wk"], a["Wv"], a["Wo"]]),
        "bqk": np.concatenate([a["bq"], a["bk"]]).reshape(4, P).T,
        "bv": a["bv"].reshape(1, D),
        "bo": a["bo"].reshape(1, D),
        "rw": a["router_w"].T,
        "w1": a["w1"].reshape(E, F, KC, P).transpose(3, 0, 2, 1).reshape(P, E * KC * F),
        "b1": a["b1"].reshape(E * FC, P).T,
        "w2": a["w2"].reshape(E, D, FC, P).transpose(3, 0, 2, 1).reshape(P, E * FC * D),
        "b2": a["b2"].reshape(1, E * D),
        "cf": f,
        "ch": h,
        "cb": b.astype(mybir.dt.np(BF16)),
    }
    nc = bacc.Bacc("TRN2", target_bir_lowering=False, num_devices=1)
    arrays, args = {}, []
    for name, val in data.items():
        arrays[name] = np.ascontiguousarray(val)
        args.append(nc.dram_tensor(name, arrays[name].shape, mybir.dt.from_np(arrays[name].dtype), kind="ExternalInput").ap())
    args.append(nc.dram_tensor("out", (T, D), F32, kind="ExternalOutput").ap())
    build(nc, *args)
    got = run_bass_kernel_spmd(nc, [arrays], core_ids=[0])
    return got.results[0]["out"].reshape(B, S, D)
```

```python
import math
from contextlib import ExitStack

import concourse.bass as bass
from concourse import mybir

F32, F16, BF16 = mybir.dt.float32, mybir.dt.float16, mybir.dt.bfloat16
I32, U32 = mybir.dt.int32, mybir.dt.uint32
ACT = mybir.ActivationFunctionType
ALU = mybir.AluOpType
AX = mybir.AxisListType

P = 128
B, S, D = 4, 2048, 256
H, HD = 16, 16
E, F = 8, 512
T = B * S
C = 128
STEPS = S // C
KC = D // P
VC = HD + 1
HC = H // KC
PAIRS = H // 2
STACK = 3 * 2 * HD
FC = F // P
MT = 256
CAP = T + MT
NT = (2 * T + E * (MT - 1)) // MT
DUMMY = E * CAP
ROWS = DUMMY + E * MT
ROW = D + 4
TOKEN, PROB1, PROB2, FIRST = range(D, ROW)
WS = 16.0
QS = 0.5
EPS = 1e-5
DEN_EPS = 1e-6 * QS * QS

C_IDENT, C_IOTA8, C_CAPS, C_TRI8, C_TILES = 0, 128, 136, 144, 208
C_POW, C_LN, C_PAD, C_TOKEN, C_END = 280, 284, 285, 287, 287 + STEPS * B
H_TRI, H_ONES, H_END = 0, 128, 256
B_IDENT, B_MASK, B_BLOCK, B_END = 0, P, P + C, P + C + KC * HC * VC


def constants():
    import numpy as np

    p = np.arange(P)
    f = np.zeros((P, C_END), np.float32)
    f[:, C_IDENT:C_IDENT + P] = np.eye(P)
    f[:, C_IOTA8:C_IOTA8 + E] = np.arange(E)
    f[:, C_CAPS:C_CAPS + E] = np.arange(E) * CAP
    f[:, C_TRI8:C_TRI8 + E * E] = (np.arange(E)[:, None] >= np.arange(E)).reshape(-1)
    f[:, C_TILES:C_TILES + NT] = np.arange(NT)
    f[:, C_POW:C_POW + B] = -0.5
    f[:, C_LN] = math.log(QS)
    f[:, C_PAD:C_PAD + 2] = T + p[:, None] + P * np.arange(2)
    f[:, C_TOKEN:] = p[:, None] + (C * np.arange(STEPS)[:, None] + S * np.arange(B)).reshape(-1)
    h = np.zeros((P, H_END), np.float16)
    h[:, H_TRI:H_TRI + P] = p[:, None] < p
    h[:, H_ONES:] = 1
    b = np.zeros((P, B_END), np.float32)
    b[:, B_IDENT:B_IDENT + P] = np.eye(P)
    b[:, B_MASK:B_MASK + C] = np.where(p[:, None] <= p, 0.0, -1e30)
    b[:, B_BLOCK:] = np.tile(np.repeat(p[:, None] // HD == np.arange(HC), VC, axis=1), (1, KC))
    return f, h, b


def build(nc, x, wqkvo, bqk, bv, bo, rw, w1, b1, w2, b2, cf, ch, cb, out):
    qk_dram = nc.dram_tensor("qk_parts", (2, 2, 4, P, B * C), F16, kind="Internal").ap()
    xg_dram = nc.dram_tensor("expert_in", (ROWS, ROW), F32, kind="Internal").ap()
    x_steps = x.rearrange("(b i p) d -> i p b d", b=B, p=C)
    out_steps = out[0:T].rearrange("(b i p) d -> i p b d", b=B, p=C)

    with ExitStack() as ctx:
        def sem(name):
            return ctx.enter_context(nc.semaphore(name))

        def sb(name, shape, dt, where=ctx):
            return where.enter_context(nc.sbuf_tensor(name, shape, dt))

        def ps(name):
            return ctx.enter_context(nc.psum_tensor(name, [P, 512], F32))

        w1s = sb("w1s", [P, 2, E * KC, F], F16)
        was = sb("was", [P, 2, 4, KC, D], F16)
        cfs = sb("cfs", [P, C_END], F32)
        chs = sb("chs", [P, H_END], F16)
        cbs = sb("cbs", [P, B_END], BF16)
        b1s = sb("b1s", [P, E * FC], F32)
        table = sb("table", [1, 2, NT], I32)
        tile_expert = sb("tile_expert", [P, NT], F32)
        pads = sb("pads", [P, 2, ROW], F32)

        att = ExitStack()
        kst = sb("kst", [P, 2, PAIRS, B * C], F16, att)
        qst = sb("qst", [P, 2, PAIRS, 2, B * C], F16, att)
        ahl = sb("ahl", [P, 2, 2, H * C], F16, att)
        vhl = sb("vhl", [P, 2, 2, B, H * VC], F16, att)
        v = sb("v", [P, 2, B, H, VC], F32, att)
        qf = sb("qf", [P, 2, 2, B * C], F32, att)
        kf = sb("kf", [P, 2, B * C], F32, att)
        qkhl = sb("qkhl", [P, 2, 4, B * C], F16, att)
        bqks = sb("bqks", [P, 4], F32, att)
        negb = sb("negb", [P, 4], F32, att)
        linb = sb("linb", [P, 4], F32, att)
        bvs = sb("bvs", [P, D], F32, att)
        bos = sb("bos", [P, D], F32, att)
        rws = sb("rws", [P, KC, E], F32, att)
        w1raw = sb("w1raw", [P, F], F32, att)
        xs = sb("xs", [P, B, D], F32, att)
        xr = sb("xr", [P, 2, B, D], F32, att)
        st1 = sb("st1", [P, B, 6], F32, att)
        mv1 = sb("mv1", [P, B, 2], F32, att)
        ve1 = sb("ve1", [P, B], F32, att)
        rs1 = sb("rs1", [P, B], F32, att)
        sh1 = sb("sh1", [P, B], F32, att)
        st2 = sb("st2", [P, B, 6], F32, att)
        mv2 = sb("mv2", [P, B, 2], F32, att)
        ve2 = sb("ve2", [P, B], F32, att)
        rs2 = sb("rs2", [P, B], F32, att)
        xn = sb("xn", [P, B, D], F32, att)
        xT = sb("xT", [P, 2, KC, B * C], F16, att)
        et = sb("et", [P, 2, B * C], F32, att)
        lt = sb("lt", [P, 2, B * C], F32, att)
        kn = sb("kn", [P, B, D], F32, att)
        state = sb("state", [P, B, KC, HC * VC], F32, att)
        ut = sb("ut", [P, KC * HC * VC], F32, att)
        rden = sb("rden", [P, 2, H], F32, att)
        at = sb("at", [P, D], F32, att)
        aT = sb("aT", [P, 2, KC, C], F16, att)
        x1 = sb("x1", [P, B, D], F32, att)
        xn2 = sb("xn2", [P, 2, B, ROW], F32, att)
        xn2T = sb("xn2T", [P, 2, KC, C], F32, att)
        lg = sb("lg", [P, B, E], F32, att)
        mx = sb("mx", [P, B, 8], F32, att)
        ix = sb("ix", [P, B, 8], U32, att)
        ixf = sb("ixf", [P, B, 2], F32, att)
        pd = sb("pd", [P, 2, B], F32, att)
        oh = sb("oh", [P, B, 2, E], F32, att)
        cnt = sb("cnt", [P, B, E], F16, att)
        ctmp = sb("ctmp", [P, E], F16, att)
        carry = sb("carry", [P, E], F16, att)
        pos = sb("pos", [P, B, E], F32, att)
        sel = sb("sel", [P, B, 2, E], F32, att)
        slf = sb("slf", [P, 2 * B], F32, att)
        cur = sb("cur", [P, 2, 2 * B], I32, att)
        tiles_f = sb("tiles_f", [P, 3, E], F32, att)
        tiles_i = sb("tiles_i", [P, E], I32, att)
        tails_i = sb("tails_i", [1, E], I32, att)
        att.close()
        past = et[:].rearrange("p a n -> p (a n)")[:, 0:NT * E].rearrange("p (t e) -> p t e", e=E)
        past_tiles = lt[:].rearrange("p a n -> p (a n)")[:, 0:NT * E].rearrange("p (t e) -> p t e", e=E)
        spare = xn[:].rearrange("p b d -> p (b d)")
        upto = spare[:, 0:E * E].rearrange("p (a b) -> p a b", a=E)
        tj = spare[:, E * E:E * E + 4 * NT].rearrange("p (a t) -> p a t", a=4)
        token_col = xn2[:].bitcast(I32)

        moe = ExitStack()
        w2s = sb("w2s", [P, 2, E, FC, D], F16, moe)
        w2raw = sb("w2raw", [P, E, FC, D], F32, moe)
        b2s = sb("b2s", [P, E, D], F32, moe)
        xg = sb("xg", [P, 2, 2, ROW], F32, moe)
        gT = sb("gT", [P, 2, 2, KC * MT], F16, moe)
        g = sb("g", [P, 2, FC, MT], F32, moe)
        ghl = sb("ghl", [P, 2, 2, FC, MT], F16, moe)
        yt = sb("yt", [P, 2, 2, D], F32, moe)
        either = sb("either", [P, 2, 2], F32, moe)
        row_prob = sb("row_prob", [P, NT, 2], F32, moe)
        row_token = sb("row_token", [P, NT, 2], I32, moe)
        to_token = sb("to_token", [P, 2, 2], I32, moe)
        moe.close()

        pF = [ps("pF0"), ps("pF1")]
        pS = [ps("pS0"), ps("pS1")]
        pO = ps("pO")
        pA = ps("pA")
        pU = ps("pU")
        pR = ps("pR")
        ident = cfs[:, C_IDENT:C_IDENT + P]
        block_mask = cbs[:, B_BLOCK:B_END]
        ident16 = cbs[:, B_IDENT:B_IDENT + P]
        mask16 = cbs[:, B_MASK:B_MASK + C].unsqueeze(1).to_broadcast([P, 4, C])
        route_bank = lambda c, b: [pR, pS[0], pS[1], pF[0]][b] if c == STEPS + 1 else pR
        LOGITS, POS = KC * C, KC * C + B * E

        consts_in = sem("consts_in")
        cf_in = sem("cf_in")
        CONSTS = 16 * 7
        passed = {nc.vector.engine: sem("passed_dve"), nc.gpsimd.engine: sem("passed_pool")}
        raw_in = sem("raw_in")
        w1_in, w1_hi, w1_lo = sem("w1_in"), sem("w1_hi"), sem("w1_lo")
        wsplit_hi = sem("wsplit_hi")
        wsplit_lo = sem("wsplit_lo")
        bias_prep = sem("bias_prep")
        ones_set = sem("ones_set")
        zero_set = sem("zero_set")
        qst_zero = sem("qst_zero")
        pads_set, pads_out = sem("pads_set"), sem("pads_out")
        x_in = sem("x_in")
        ln1_st, ln1_mv, ln1_ve, ln1_rs = sem("ln1_st"), sem("ln1_mv"), sem("ln1_ve"), sem("ln1_rs")
        ln1_sh = sem("ln1_sh")
        ln2_st, ln2_mv, ln2_ve, ln2_rs = sem("ln2_st"), sem("ln2_mv"), sem("ln2_ve"), sem("ln2_rs")
        xn_done, xr_in, xr_done = sem("xn_done"), sem("xr_in"), sem("xr_done")
        xT_ps, xT_hi, xT_lo = sem("xT_ps"), sem("xT_hi"), sem("xT_lo")
        qk_ps, qk_neg, qk_lin, qk_f = sem("qk_ps"), sem("qk_neg"), sem("qk_lin"), sem("qk_f")
        qk_hi, qk_lo, qk_out = sem("qk_hi"), sem("qk_lo"), sem("qk_out")
        stack_in = [sem("stack_in0"), sem("stack_in1")]
        v_ps, v_done, v_hi, v_lo = sem("v_ps"), sem("v_done"), sem("v_hi"), sem("v_lo")
        kn_ps, kn_done = sem("kn_ps"), sem("kn_done")
        sc_ps, sc_hi, sc_lo = sem("sc_ps"), sem("sc_hi"), sem("sc_lo")
        o_ps, den_add, den_rec, at_done = sem("o_ps"), sem("den_add"), sem("den_rec"), sem("at_done")
        u_ps, ut_done, state_new = sem("u_ps"), sem("ut_done"), sem("state_new")
        aT_ps, aT_hi, aT_lo, wo_ps = sem("aT_ps"), sem("aT_hi"), sem("aT_lo"), sem("wo_ps")
        x1_done, x1_out = sem("x1_done"), sem("x1_out")
        xn2_done, xn2T_ps, xn2T_done, lg_ps = sem("xn2_done"), sem("xn2T_ps"), sem("xn2T_done"), sem("lg_ps")
        rt = sem("rt")
        top_gap, top_exp = sem("top_gap"), sem("top_exp")
        cnt_done, carry_done, pos_ps = sem("cnt_done"), sem("carry_done"), sem("pos_ps")
        slot_done = sem("slot_done")
        scat_out = [sem("scat_out0"), sem("scat_out1")]
        tot_ps, tail_done, tail_out, tab = sem("tot_ps"), sem("tail_done"), sem("tail_out"), sem("tab")
        TAB = 14
        RT = 11

        def front_of(j, c):
            return 2 * j + c, j + c // 2

        LOOP0, LOOP1 = 5, 15
        END = STEPS + 3

        def iterations(engine, body):
            body(0, 0)
            body(0, 1, back=False)
            body(0, 1, front=False)
            for c in range(2, LOOP0):
                body(0, c)
            with engine.Fori(0, (LOOP1 - LOOP0) // 2) as j:
                for c in (LOOP0, LOOP0 + 1):
                    body(j, c)
            for c in range(LOOP1, END):
                body(0, c)

        def real(j, c):
            return not isinstance(j, int) or 0 <= c < STEPS

        xg_in = [sem("xg_in0"), sem("xg_in1")]
        w2_in = [sem(f"w2_in{n}") for n in range(E // 2)]
        b2_in, w2_hi, w2_lo = sem("b2_in"), sem("w2_hi"), sem("w2_lo")
        gt_ps, gt_hi, gt_lo, h_ps = sem("gt_ps"), sem("gt_hi"), sem("gt_lo"), sem("h_ps")
        gelu, g_hi, g_lo, y_ps = sem("gelu"), sem("g_hi"), sem("g_lo"), sem("y_ps")
        which, meta, y_biased, y_done = sem("which"), sem("meta"), sem("y_biased"), sem("y_done")
        token_copy, added = sem("token_copy"), sem("added")
        W2Q = 4
        W2E = E // W2Q
        rows_T = [pR, pF[0]]
        hidden = [pS, [pO, pA]]
        y_bank = [pU, pF[1]]

        def tiles(engine, body, first=-2):
            for c in range(first, 2):
                body(0, c)
            with engine.Fori(0, (NT - 5) // 2) as j:
                for c in (2, 3):
                    body(j, c)
            for c in range(2 + (NT - 5) // 2 * 2, NT):
                body(0, c)

        def is_tile(j, c):
            return not isinstance(j, int) or 0 <= c < NT

        def feature_rows(m, par):
            return qf[:, par, m] if m < 2 else kf[:, m - 2]

        def carry_wait(engine):
            engine.sem_inc(passed[engine.engine], 1)

        block = ctx.enter_context(nc.Block())

        @block.sync
        def _(sp):
            sp.dma_start(xs[:], x_steps[0]).then_inc(x_in, 16)
            sp.dma_start(cfs[:], cf).then_inc(cf_in, 16)
            sp.dma_start(bqks[:], bqk).then_inc(consts_in, 16)
            sp.dma_start(chs[:], ch).then_inc(consts_in, 16)
            sp.dma_start(bvs[:], bv.partition_broadcast(P)).then_inc(consts_in, 16)
            sp.dma_start(bos[:], bo.partition_broadcast(P)).then_inc(consts_in, 16)
            sp.dma_start(rws[:], rw.rearrange("(k p) e -> p k e", p=P)).then_inc(consts_in, 16)
            sp.dma_start(b1s[:], b1).then_inc(consts_in, 16)
            sp.dma_start(w1raw[:], w1[:, 0:F]).then_inc(w1_in, 16)

            def body(j, c, front=True, back=True):
                i, _ = front_of(j, c)
                r, _ = front_of(j, c - 2)
                fr, ro, nx = front and real(j, c), real(j, c - 2), front and real(j, c + 1)
                for n in range(0 if c == 1 else 2 if c == 0 else 1 if nx else 0):
                    sp.wait_ge(xn_done, 4 * (i + n) + 4)
                    sp.dma_start(xs[:], x_steps[bass.ds(i + n + 1, 1)].rearrange("i p b d -> p (i b) d")).then_inc(x_in, 16)
                if ro:
                    sp.wait_ge(x1_done, 4 * r + 4)
                    sp.dma_start(out_steps[bass.ds(r, 1)].rearrange("i p b d -> p (i b) d"), x1[:]).then_inc(x1_out, 16)
                if fr:
                    par = c % 2
                    sp.dma_start(xr[:, par], x_steps[bass.ds(i, 1)].rearrange("i p b d -> p (i b) d")).then_inc(xr_in, 16)
                    sp.wait_ge(qk_hi, 4 * i + 4)
                    sp.wait_ge(qk_lo, 4 * i + 4)
                    if c >= 2:
                        sp.wait_ge(stack_in[par], 144 * (j + c // 2))
                    sp.dma_start(qk_dram[par].rearrange("h m p n -> p (h m) n"),
                                 qkhl[:].rearrange("p h m n -> p (h m) n")).then_inc(qk_out, 16)
                    sp.wait_ge(qk_out, 16 * i + 16)
                    if c >= 2:
                        sp.wait_ge(sc_ps, 16 * (i - 1))
                    else:
                        sp.wait_ge(wsplit_lo, 4)
                        sp.wait_ge(qst_zero, 2)
                    rows = qk_dram[par].rearrange("h (t k) p n -> h t (k p) n", t=2)
                    for part in range(3):
                        src = rows[part // 2, 1].rearrange("(a r) n -> r a n", r=2 * HD)
                        sp.dma_start(kst[2 * HD * part:2 * HD * (part + 1), par], src).then_inc(stack_in[par], 16)
                        src = rows[part % 2, 0].rearrange("(a e d) n -> e d a n", e=2, d=HD)
                        for e in range(2):
                            r0 = 2 * HD * part + HD * e
                            sp.dma_start(qst[r0:r0 + HD, par, :, e], src[e]).then_inc(stack_in[par], 16)
                if fr and nx:
                    sp.wait_ge(w1_lo, i + 1)
                    sp.dma_start(w1raw[:], w1[:, bass.ds(i * F + F, F)]).then_inc(w1_in, 16)
                if c == 2:
                    sp.wait_ge(pads_set, 2)
                    for n in range(E):
                        sp.dma_start(xg_dram[DUMMY + n * MT:DUMMY + (n + 1) * MT].rearrange("(s p) d -> p s d", p=P),
                                     pads[:]).then_inc(pads_out, 16)
                    sp.dma_start(out[T:T + MT].rearrange("(s p) d -> p s d", p=P), pads[:, :, 0:D]).then_inc(pads_out, 16)
                if c == STEPS:
                    for n in range(W2Q):
                        sp.wait_ge(*((sc_ps, 16 * STEPS) if n < W2Q // 2 else (o_ps, 4 * STEPS)))
                        sp.dma_start(w2raw[:, n * W2E:(n + 1) * W2E].rearrange("p e f d -> p (e f d)"),
                                     w2[:, n * W2E * FC * D:(n + 1) * W2E * FC * D]).then_inc(w2_in[n], 16)
                    sp.wait_ge(u_ps, 4 * STEPS)
                    sp.dma_start(b2s[:].rearrange("p e d -> p (e d)"), b2.partition_broadcast(P)).then_inc(b2_in, 16)

            iterations(sp, body)

            sp.wait_ge(tail_done, 1)
            for e in range(E):
                row = sp.value_load(tails_i[0:1, e:e + 1], min_val=0, max_val=ROWS - MT)
                sp.dma_start(xg_dram[bass.ds(row, MT)].rearrange("(s p) d -> p s d", p=P), pads[:]).then_inc(tail_out, 16)
            sp.wait_ge(tab, TAB)
            sp.wait_ge(tail_out, 16 * E)
            sp.wait_ge(pads_out, 16 * (E + 1))
            for n in range(2):
                sp.wait_ge(scat_out[n], 128 * STEPS // 2)

            def load(j, c):
                t, th = front_of(j, c)
                if not is_tile(j, c):
                    return
                row = sp.value_load(table[0:1, 0, bass.ds(t, 1)], min_val=0, max_val=ROWS - MT)
                if c >= 2:
                    sp.wait_ge(gt_ps, t - 1)
                    sp.wait_ge(meta, t - 1)
                sp.dma_start(xg[:, c % 2], xg_dram[bass.ds(row, MT), :].rearrange("(s p) d -> p s d", p=P)).then_inc(xg_in[c % 2], 16)

            tiles(sp, load, 0)

        @block.tensor
        def _(pe):
            def split3(out, lhs, rhs, n, first=True):
                terms = [(a, b_, k) for a, b_ in ((0, 0), (0, 1), (1, 0)) for k in range(n)]
                for t, (a, b_, k) in enumerate(terms):
                    mm = nc.tensor.matmul(out, lhs(a, k), rhs(b_, k), start=(t == 0), stop=(t == len(terms) - 1))
                return mm

            def body(j, c, front=True, back=True):
                i, _ = front_of(j, c)
                s, _ = front_of(j, c - 1)
                r, _ = front_of(j, c - 2)
                q, _ = front_of(j, c - 3)
                fr, bk, ro, sc = front and real(j, c), back and real(j, c - 1), real(j, c - 2), real(j, c - 3)
                turn_k = front and real(j, c - 1)
                par, sp_ = c % 2, (c - 1) % 2
                first_s, first_r = c == 1, c == 2

                def x_transposes(k):
                    if k == 0:
                        pe.wait_ge(xn_done, 4 * i + 4)
                    if c >= 1:
                        pe.wait_ge(v_done, 2 * i - 1 + k)
                    for b in range(B):
                        mm = nc.tensor.transpose(pF[k][:, b * C:(b + 1) * C], xn[:, b, k * P:(k + 1) * P], ident)
                    mm.then_inc(xT_ps, 1)

                def project(m):
                    if m == 0:
                        pe.wait_ge(xT_lo, 2 * i + 2)
                    if m >= 2:
                        pe.wait_ge(qk_lin, 4 * i + m - 1)
                    w, k0 = m // 2, (m % 2) * P
                    if c == 0 and m % 2 == 0:
                        pe.wait_ge(wsplit_lo, w + 1)
                    split3(pF[m % 2][:], lambda a, k: was[:, a, w, k, k0:k0 + P], lambda a, k: xT[:, a, k], KC).then_inc(qk_ps, 1)

                def values(n):
                    pe.wait_ge(qk_lin, 4 * i + 3 + n)
                    if c == 0 and n == 0:
                        pe.wait_ge(wsplit_lo, 4)
                    for b in (2 * n, 2 * n + 1):
                        mm = split3(pF[n][:, (b % 2) * D:(b % 2 + 1) * D], lambda a, k: xT[:, a, k, b * C:(b + 1) * C],
                                    lambda a, k: was[:, a, 2, k], KC)
                    mm.then_inc(v_ps, 1)

                def k_rows(n):
                    if n == 0:
                        pe.wait_ge(qk_f, 4 * s + 4)
                        if not first_s:
                            pe.wait_ge(ut_done, 4 * s)
                    else:
                        pe.wait_ge(kn_done, 2 * s + 1)
                    for b in (2 * n, 2 * n + 1):
                        for k in range(KC):
                            c0 = (b % 2) * D + k * P
                            mm = nc.tensor.transpose(pU[:, c0:c0 + P], kf[:, k, b * C:(b + 1) * C], ident)
                    mm.then_inc(kn_ps, 1)

                def scores(b, n):
                    g = 16 * s + 4 * b + n
                    if b == n == 0:
                        pe.wait_ge(stack_in[sp_], 144 * (j + (c - 1) // 2 + 1))
                    if not (first_s and 4 * b + n < 2):
                        pe.wait_ge(sc_lo, g - 1)
                    o = pS[n % 2]
                    nc.tensor.matmul(o[:], ident16, mask16, start=True, stop=False, skip_group_check=True)
                    for e in range(2):
                        pr = 2 * n + e
                        mm = nc.tensor.matmul(o[:, e * 2 * C:(e + 1) * 2 * C], kst[0:STACK, sp_, pr, b * C:(b + 1) * C],
                                              qst[0:STACK, sp_, pr, :, b * C:(b + 1) * C], start=False, stop=(e == 1),
                                              skip_group_check=True)
                    mm.then_inc(sc_ps, 1)

                def attend(b):
                    g = 4 * s + b
                    if first_s:
                        pe.wait_ge(zero_set, 1)
                    else:
                        pe.wait_ge(state_new, 4 * s - 3 + b)
                    if not (first_s and b == 0):
                        pe.wait_ge(at_done, g)
                    for k in range(KC):
                        nc.tensor.matmul(pO[:, k * HC * VC:(k + 1) * HC * VC], qf[:, sp_, k, b * C:(b + 1) * C], state[:, b, k],
                                         start=(k == 0), stop=False, skip_group_check=True)
                    pe.wait_ge(sc_lo, 4 * g + 4)
                    pe.wait_ge(v_lo, s + 1)
                    for h in range(H):
                        for a, b_ in ((0, 0), (0, 1), (1, 0)):
                            mm = nc.tensor.matmul(pO[:, h * VC:(h + 1) * VC], ahl[:, b % 2, a, h * C:(h + 1) * C],
                                                  vhl[:, sp_, b_, b, h * VC:(h + 1) * VC], start=False,
                                                  stop=(h == H - 1 and a == 1), skip_group_check=True)
                    mm.then_inc(o_ps, 1)
                    pe.wait_ge(kn_done, 2 * s + 2)
                    if not (first_s and b == 0):
                        pe.wait_ge(ut_done, g)
                    for k in range(KC):
                        mm = nc.tensor.matmul(pU[:, k * HC * VC:(k + 1) * HC * VC], kn[:, b, k * P:(k + 1) * P],
                                              v[:, sp_, b, k * HC:(k + 1) * HC].rearrange("p h c -> p (h c)"), start=True, stop=True)
                    mm.then_inc(u_ps, 1)

                def out_transpose(s, b):
                    g = 4 * s + b
                    pe.wait_ge(at_done, g + 1)
                    for k in range(KC):
                        mm = nc.tensor.transpose(pA[:, k * C:(k + 1) * C], at[:, k * P:(k + 1) * P], ident)
                    mm.then_inc(aT_ps, 1)

                def out_project(s, b):
                    g = 4 * s + b
                    pe.wait_ge(aT_lo, g + 1)
                    if not (first_s and b == 0):
                        pe.wait_ge(x1_done, g)
                    split3(pA[:, D:2 * D], lambda a, k: aT[:, a, k], lambda a, k: was[:, a, 3, k], KC).then_inc(wo_ps, 1)

                def route_transpose(b):
                    g = 4 * r + b
                    pe.wait_ge(xn2_done, g + 1)
                    if b == 0 and not first_r:
                        pe.wait_ge(slot_done, r)
                    for k in range(KC):
                        mm = nc.tensor.transpose(route_bank(c, b)[:, k * C:(k + 1) * C], xn2[:, c % 2, b, k * P:(k + 1) * P], ident)
                    mm.then_inc(xn2T_ps, 1)

                def route_logits(b):
                    g = 4 * r + b
                    pe.wait_ge(xn2T_done, g + 1)
                    for k in range(KC):
                        mm = nc.tensor.matmul(pR[:, LOGITS + b * E:LOGITS + (b + 1) * E], xn2T[:, b % 2, k], rws[:, k],
                                              start=(k == 0), stop=(k == KC - 1))
                    mm.then_inc(lg_ps, 1)

                def route_positions():
                    pe.wait_ge(cnt_done, q + 1)
                    if c != 3:
                        pe.wait_ge(carry_done, q)
                    else:
                        pe.wait_ge(zero_set, 2)
                    o = pR[:, POS:POS + B * E]
                    nc.tensor.matmul(o, chs[:, H_TRI:H_TRI + P], cnt[:].rearrange("p b e -> p (b e)"), start=True, stop=False,
                                     skip_group_check=True)
                    for d in range(1, B):
                        nc.tensor.matmul(o[:, d * E:], chs[:, H_ONES:H_ONES + P],
                                         cnt[:, 0:B - d].rearrange("p b e -> p (b e)"), start=False, stop=False,
                                         skip_group_check=True)
                    nc.tensor.matmul(o, chs[:, H_ONES:H_ONES + P], carry[:].unsqueeze(1).to_broadcast([P, B, E]), start=False,
                                     stop=True, skip_group_check=True).then_inc(pos_ps, 1)

                if fr:
                    x_transposes(0)
                    x_transposes(1)
                if bk:
                    scores(0, 0)
                if ro:
                    out_transpose(r, 3)
                if bk:
                    scores(0, 1)
                if turn_k:
                    k_rows(0)
                if sc:
                    route_positions()
                if c == STEPS + 1:
                    out_project(r, 3)
                    for b in range(B):
                        route_transpose(b)
                    for b in range(B):
                        route_logits(b)
                    return
                if fr:
                    project(0)
                if bk:
                    scores(0, 2)
                if ro:
                    out_project(r, 3)
                if fr:
                    project(1)
                if bk:
                    scores(0, 3)
                if turn_k:
                    k_rows(1)
                if bk:
                    scores(1, 0)
                if fr:
                    project(2)
                if bk:
                    attend(0)
                    scores(1, 1)
                if fr:
                    project(3)
                if bk:
                    out_transpose(s, 0)
                    scores(1, 2)
                if ro:
                    route_transpose(0)
                if bk:
                    scores(1, 3)
                    out_project(s, 0)
                if ro:
                    route_logits(0)
                    route_transpose(1)
                if bk:
                    scores(2, 0)
                    attend(1)
                    scores(2, 1)
                if ro:
                    route_logits(1)
                    route_transpose(2)
                if fr:
                    values(0)
                if bk:
                    out_transpose(s, 1)
                    scores(2, 2)
                if ro:
                    route_logits(2)
                    route_transpose(3)
                if bk:
                    scores(2, 3)
                    out_project(s, 1)
                    scores(3, 0)
                    scores(3, 1)
                    attend(2)
                if ro:
                    route_logits(3)
                if bk:
                    scores(3, 2)
                    out_transpose(s, 2)
                    scores(3, 3)
                if fr:
                    values(1)
                if bk:
                    out_project(s, 2)
                    attend(3)

            pe.wait_ge(cf_in, 16)
            pe.wait_ge(consts_in, CONSTS)
            iterations(pe, body)
            pe.wait_ge(carry_done, STEPS)
            pe.wait_ge(slot_done, STEPS)
            nc.tensor.matmul(pR[:, 0:E], chs[:, H_ONES:H_ONES + P], carry[:], start=True, stop=True).then_inc(tot_ps, 1)

            def tile(j, c):
                t, th = front_of(j, c)

                def hidden_layer():
                    p1 = (c + 1) % 2
                    e = pe.value_load(table[0:1, 1, bass.ds(t + 1, 1)], min_val=0, max_val=E - 1)
                    pe.wait_ge(gt_lo, t + 2)
                    if c == -1:
                        pe.wait_ge(w1_lo, E * KC)
                    if c + 1 >= 2:
                        pe.wait_ge(gelu, 4 * t)
                    for f in range(FC):
                        mm = split3(hidden[p1][f // 2][:, (f % 2) * MT:(f % 2 + 1) * MT],
                                    lambda a, k: w1s[:, a, bass.ds(e * KC + k, 1), f * P:(f + 1) * P].rearrange("p e f -> p (e f)"),
                                    lambda a, k: gT[:, p1, a, k * MT:(k + 1) * MT], KC)
                        if f % 2:
                            mm.then_inc(h_ps, 1)

                def turn():
                    pe.wait_ge(xg_in[c % 2], 16 * (j + (c + 2) // 2 + 1))
                    if c + 2 >= 2:
                        pe.wait_ge(gt_lo, t + 1)
                    for k in range(KC):
                        for s in range(MT // P):
                            mm = nc.tensor.transpose(rows_T[c % 2][:, k * MT + s * P:k * MT + (s + 1) * P],
                                                     xg[:, c % 2, s, k * P:(k + 1) * P], ident)
                    mm.then_inc(gt_ps, 1)

                def second_layer():
                    e = pe.value_load(table[0:1, 1, bass.ds(t, 1)], min_val=0, max_val=E - 1)
                    pe.wait_ge(g_lo, t + 1)
                    if c == 0:
                        pe.wait_ge(w2_lo, W2Q)
                    if c >= 2:
                        pe.wait_ge(y_done, t - 1)
                    for s in range(MT // P):
                        mm = split3(y_bank[c % 2][:, s * D:(s + 1) * D], lambda a, f: ghl[:, c % 2, a, f, s * P:(s + 1) * P],
                                    lambda a, f: w2s[:, a, bass.ds(e, 1), f].rearrange("p e d -> p (e d)"), FC)
                    mm.then_inc(y_ps, 1)

                if is_tile(j, c + 1):
                    hidden_layer()
                if is_tile(j, c + 2):
                    turn()
                if is_tile(j, c):
                    second_layer()

            pe.wait_ge(tab, TAB)
            tiles(pe, tile)

        @block.scalar
        def _(act):
            raw = kst[:].bitcast(F32).rearrange("p a b c -> p (a b c)")[:, 0:4 * KC * D]
            act.dma_start(cbs[:], cb).then_inc(consts_in, 16)
            act.dma_start(raw.rearrange("p (w n) -> p w n", w=4 * KC),
                          wqkvo.rearrange("w (k p) n -> p (w k) n", p=P)).then_inc(raw_in, 16)
            def normalise(i, half, first=False):
                if half == 0:
                    act.wait_ge(x_in, 16 * i + 16)
                    act.wait_ge(ln1_sh, i + 1)
                    if not first:
                        act.wait_ge(xT_ps, 2 * i)
                for b in (2 * half, 2 * half + 1):
                    nc.scalar.activation(xn[:, b], xs[:, b], ACT.Identity, bias=sh1[:, b:b + 1], scale=rs1[:, b:b + 1]).then_inc(xn_done, 1)

            for half in range(2):
                normalise(0, half, first=True)
            act.wait_ge(raw_in, 16)
            for w in range(4):
                nc.scalar.activation(was[:, 0, w], raw.rearrange("p (w k n) -> p w k n", w=4, k=KC)[:, w], ACT.Copy,
                                     scale=WS).then_inc(wsplit_hi, 1)
            act.wait_ge(cf_in, 16)
            act.wait_ge(consts_in, CONSTS)

            def body(j, c, front=True, back=True):
                i, _ = front_of(j, c)
                s, _ = front_of(j, c - 1)
                r, _ = front_of(j, c - 2)
                q, _ = front_of(j, c - 3)
                fr, bk, ro, sc = front and real(j, c), back and real(j, c - 1), real(j, c - 2), real(j, c - 3)
                turn_k, nx = front and real(j, c - 1), front and real(j, c + 1)
                par = c % 2

                def kn_rows(n):
                    act.wait_ge(kn_ps, 2 * s + 1 + n)
                    if c >= 2:
                        act.wait_ge(u_ps, 4 * s)
                    nc.scalar.activation(kn[:, 2 * n:2 * n + 2].rearrange("p b d -> p (b d)"), pU[:], ACT.Copy).then_inc(kn_done, 1)

                def score_hi(b, n):
                    g = 16 * s + 4 * b + n
                    act.wait_ge(sc_ps, g + 1)
                    if n == 0 and not (c == 1 and b < 2):
                        act.wait_ge(o_ps, 4 * s + b - 1)
                    nc.scalar.activation(ahl[:, b % 2, 0, n * 4 * C:(n + 1) * 4 * C], pS[n % 2][:], ACT.Relu).then_inc(sc_hi, 1)

                def x_hi(k):
                    act.wait_ge(xT_ps, 2 * i + k + 1)
                    if c >= 1:
                        act.wait_ge(v_ps, 2 * i)
                    nc.scalar.activation(xT[:, 0, k], pF[k][:], ACT.Copy).then_inc(xT_hi, 1)

                def feature_in(m):
                    act.wait_ge(qk_ps, 4 * i + m + 1)
                    if not (c == 0 and m < 2):
                        act.wait_ge(qk_f, 4 * i + m - 1)
                    e_, l_ = et[:, m % 2], lt[:, m % 2]
                    nc.scalar.activation(e_, pF[m % 2][:], ACT.Relu, bias=negb[:, m:m + 1], scale=-1.0 / WS).then_inc(qk_neg, 1)
                    nc.scalar.activation(l_, pF[m % 2][:], ACT.Relu, bias=linb[:, m:m + 1], scale=QS / WS).then_inc(qk_lin, 1)

                def feature_exp(m):
                    e_ = et[:, m % 2]
                    act.wait_ge(qk_neg, 8 * i + 2 * m + 1)
                    nc.scalar.activation(e_, e_, ACT.Exp, bias=cfs[:, C_LN:C_LN + 1], scale=-1.0).then_inc(qk_neg, 1)

                def feature(m):
                    feature_in(m)
                    feature_exp(m)

                def qk_high(m):
                    act.wait_ge(qk_f, 4 * i + m + 1)
                    if c >= 1:
                        act.wait_ge(qk_out, 16 * i)
                    nc.scalar.activation(qkhl[:, 0, m], feature_rows(m, par), ACT.Copy).then_inc(qk_hi, 1)

                def v_high():
                    act.wait_ge(v_done, 2 * i + 2)
                    if c >= 2:
                        act.wait_ge(o_ps, 4 * (i - 1))
                    nc.scalar.activation(vhl[:, par, 0].rearrange("p b n -> p (b n)"),
                                         v[:, par].rearrange("p b h c -> p (b h c)"), ACT.Copy).then_inc(v_hi, 1)

                def row_copy(b):
                    g = 4 * r + b
                    act.wait_ge(xn2T_ps, g + 1)
                    if not (c == 2 and b < 2):
                        act.wait_ge(lg_ps, g - 1)
                    nc.scalar.activation(xn2T[:, b % 2].rearrange("p k n -> p (k n)"), route_bank(c, b)[:, 0:KC * C],
                                         ACT.Copy).then_inc(xn2T_done, 1)

                def out_hi(s, b):
                    g = 4 * s + b
                    act.wait_ge(aT_ps, g + 1)
                    nc.scalar.activation(aT[:, 0].rearrange("p k n -> p (k n)"), pA[:, 0:KC * C], ACT.Copy).then_inc(aT_hi, 1)

                def w1_high():
                    act.wait_ge(w1_in, 16 * i + 16)
                    nc.scalar.activation(w1s[:, 0, bass.ds(i, 1)].rearrange("p i f -> p (i f)"), w1raw[:], ACT.Copy,
                                         scale=WS).then_inc(w1_hi, 1)

                if fr:
                    x_hi(0)
                    x_hi(1)
                if bk:
                    score_hi(0, 0)
                if ro:
                    out_hi(r, 3)
                if bk:
                    score_hi(0, 1)
                if turn_k:
                    kn_rows(0)
                if sc:
                    act.wait_ge(top_gap, q + 1)
                    nc.scalar.activation(pd[:, 1], pd[:, 0], ACT.Exp).then_inc(top_exp, 1)
                if c == STEPS + 1:
                    w2_high(0)
                    w2_high(1)
                if fr and c >= 2:
                    w1_high()
                if fr:
                    feature(0)
                if bk:
                    score_hi(0, 2)
                if fr:
                    feature(1)
                if bk:
                    score_hi(0, 3)
                if turn_k:
                    kn_rows(1)
                if fr:
                    qk_high(0)
                if bk:
                    score_hi(1, 0)
                if fr:
                    feature(2)
                    qk_high(1)
                if bk:
                    score_hi(1, 1)
                if bk:
                    out_hi(s, 0)
                    score_hi(1, 2)
                if ro:
                    row_copy(0)
                if bk:
                    score_hi(1, 3)
                if fr:
                    feature(3)
                    qk_high(2)
                if bk:
                    score_hi(2, 0)
                if ro:
                    row_copy(1)
                if fr:
                    qk_high(3)
                if bk:
                    score_hi(2, 1)
                if ro:
                    row_copy(2)
                if bk:
                    out_hi(s, 1)
                    score_hi(2, 2)
                if ro:
                    row_copy(3)
                if bk:
                    score_hi(2, 3)
                if bk:
                    score_hi(3, 0)
                    score_hi(3, 1)
                if nx:
                    normalise(i + 1, 0)
                if bk:
                    score_hi(3, 2)
                    out_hi(s, 2)
                    score_hi(3, 3)
                if nx:
                    normalise(i + 1, 1)
                if fr:
                    v_high()
                if fr and c < 2:
                    w1_high()

            def w2_high(n):
                act.wait_ge(w2_in[n], 16)
                nc.scalar.activation(w2s[:, 0, n * W2E:(n + 1) * W2E].rearrange("p e f d -> p (e f d)"),
                                     w2raw[:, n * W2E:(n + 1) * W2E].rearrange("p e f d -> p (e f d)"), ACT.Copy,
                                     scale=WS).then_inc(w2_hi, 1)

            iterations(act, body)
            for n in range(2, W2Q):
                w2_high(n)

            def tile(j, c):
                t, _ = front_of(j, c)
                if is_tile(j, c + 1):
                    p1 = (c + 1) % 2
                    e = act.value_load(table[0:1, 1, bass.ds(t + 1, 1)], min_val=0, max_val=E - 1)
                    if c + 1 >= 2:
                        act.wait_ge(g_lo, t)
                    for f in range(FC):
                        act.wait_ge(h_ps, 2 * t + 3 + f // 2)
                        nc.scalar.activation(g[:, p1, f], hidden[p1][f // 2][:, (f % 2) * MT:(f % 2 + 1) * MT], ACT.Gelu,
                                             bias=b1s[:, bass.ds(e * FC + f, 1)], scale=1.0 / WS).then_inc(gelu, 1)
                if is_tile(j, c + 2):
                    act.wait_ge(gt_ps, t + 3)
                    if c + 2 >= 2:
                        act.wait_ge(h_ps, 2 * t + 2)
                    nc.scalar.activation(gT[:, c % 2, 0], rows_T[c % 2][:], ACT.Copy).then_inc(gt_hi, 1)
                if is_tile(j, c + 1):
                    act.wait_ge(gelu, 4 * t + 8)
                    if c + 1 >= 2:
                        act.wait_ge(y_ps, t)
                    nc.scalar.activation(ghl[:, p1, 0].rearrange("p f n -> p (f n)"), g[:, p1].rearrange("p f n -> p (f n)"),
                                         ACT.Copy).then_inc(g_hi, 1)

            act.wait_ge(tab, TAB)
            tiles(act, tile)

        @block.vector
        def _(dve):
            V = nc.vector
            V.memset(state[:].rearrange("p a b c -> p (a b c)"), 0.0).then_inc(zero_set, 1)
            V.memset(carry[:], 0.0).then_inc(zero_set, 1)
            for par in range(2):
                V.memset(v[:, par].rearrange("p b h c -> p (b h) c")[:, :, HD:VC], 1.0).then_inc(ones_set, 1)

            def norm_moments(i, st, mv, ve, sems):
                dve.wait_ge(sems[0], 4 * i + 4)
                carry_wait(dve)
                for b in range(B):
                    V.bn_aggr(mv[:, b], st[:, b]).then_inc(sems[1], 1)
                dve.wait_ge(sems[1], 4 * i + 4)
                V.tensor_scalar(ve[:], mv[:, :, 1], EPS, None, ALU.add).then_inc(sems[2], 1)

            def stats2(s, b):
                dve.wait_ge(x1_done, 4 * s + b + 1)
                V.bn_stats(st2[:, b], x1[:, b]).then_inc(ln2_st, 1)

            def norm1_stats(i):
                dve.wait_ge(x_in, 16 * i + 16)
                for b in range(B):
                    V.bn_stats(st1[:, b], xs[:, b]).then_inc(ln1_st, 1)

            def norm1_shift(i, first=False):
                dve.wait_ge(ln1_rs, i + 1)
                if not first:
                    dve.wait_ge(xn_done, 4 * i)
                V.scalar_tensor_tensor(sh1[:], mv1[:, :, 0], -1.0, rs1[:], ALU.mult, ALU.mult).then_inc(ln1_sh, 1)

            def body(j, c, front=True, back=True):
                i, _ = front_of(j, c)
                s, _ = front_of(j, c - 1)
                r, rh = front_of(j, c - 2)
                q, qh = front_of(j, c - 3)
                fr, bk, ro, sc = front and real(j, c), back and real(j, c - 1), real(j, c - 2), real(j, c - 3)
                nx = front and real(j, c + 1)
                par, sp_, rp, qp = c % 2, (c - 1) % 2, c % 2, (c - 3) % 2

                def score_lo(b, n):
                    dve.wait_ge(sc_hi, 16 * s + 4 * b + n + 1)
                    cols = slice(n * 4 * C, (n + 1) * 4 * C)
                    V.scalar_tensor_tensor(ahl[:, b % 2, 1, cols], pS[n % 2][:], 0.0, ahl[:, b % 2, 0, cols], ALU.max,
                                           ALU.subtract).then_inc(sc_lo, 1)

                def x_lo(k):
                    dve.wait_ge(xT_hi, 2 * i + k + 1)
                    V.tensor_tensor(xT[:, 1, k], pF[k][:], xT[:, 0, k], ALU.subtract).then_inc(xT_lo, 1)

                def norm2_apply(half):
                    if half == 0:
                        dve.wait_ge(ln2_rs, r + 1)
                        if c >= 4:
                            dve.wait_ge(scat_out[rp], 128 * rh)
                    for b in (2 * half, 2 * half + 1):
                        V.tensor_scalar(xn2[:, rp, b, 0:D], x1[:, b], mv2[:, b, 0:1], rs2[:, b:b + 1], ALU.subtract,
                                        ALU.mult).then_inc(xn2_done, 1)

                def attention(b):
                    g = 4 * s + b
                    dve.wait_ge(o_ps, g + 1)
                    o = pO[:, 0:H * VC].rearrange("p (h c) -> p h c", c=VC)
                    V.tensor_scalar(rden[:, 0], o[:, :, HD], DEN_EPS, None, ALU.add).then_inc(den_add, 1)
                    dve.wait_ge(den_add, g + 1)
                    V.reciprocal(rden[:, 1], rden[:, 0]).then_inc(den_rec, 1)
                    dve.wait_ge(den_rec, g + 1)
                    if not (c == 1 and b == 0):
                        dve.wait_ge(aT_ps, g)
                    V.tensor_tensor(at[:].rearrange("p (h c) -> p h c", c=HD), o[:, :, 0:HD],
                                    rden[:, 1].unsqueeze(2).to_broadcast([P, H, HD]), ALU.mult).then_inc(at_done, 1)

                def state_part(b):
                    g = 4 * s + b
                    dve.wait_ge(u_ps, g + 1)
                    if not (c == 1 and b == 0):
                        dve.wait_ge(state_new, g)
                    V.tensor_tensor(ut[:], pU[:, 0:KC * HC * VC], block_mask, ALU.mult).then_inc(ut_done, 1)

                def out_lo(s, b):
                    g = 4 * s + b
                    dve.wait_ge(aT_hi, g + 1)
                    V.tensor_tensor(aT[:, 1].rearrange("p k n -> p (k n)"), pA[:, 0:KC * C], aT[:, 0].rearrange("p k n -> p (k n)"),
                                    ALU.subtract).then_inc(aT_lo, 1)

                def residual(s, b, buffer):
                    g = 4 * s + b
                    dve.wait_ge(wo_ps, g + 1)
                    if b == 0:
                        dve.wait_ge(xr_done, s + 1)
                        if c >= 2:
                            dve.wait_ge(x1_out, 16 * s)
                            dve.wait_ge(xn2_done, 4 * s)
                    V.scalar_tensor_tensor(x1[:, b], pA[:, D:2 * D], 1.0 / WS, xr[:, buffer, b], ALU.mult, ALU.add).then_inc(x1_done, 1)
                    stats2(s, b)

                def values(n):
                    dve.wait_ge(v_ps, 2 * i + 1 + n)
                    if c >= 2 and n == 0:
                        dve.wait_ge(u_ps, 4 * (i - 1))
                    V.scalar_tensor_tensor(v[:, par, 2 * n:2 * n + 2, :, 0:HD],
                                           pF[n][:].rearrange("p (b h c) -> p b h c", b=2, h=H), 1.0 / WS,
                                           bvs[:].rearrange("p (h c) -> p h c", h=H).unsqueeze(1).to_broadcast([P, 2, H, HD]),
                                           ALU.mult, ALU.add).then_inc(v_done, 1)

                links = [0]

                def link(step, ins):
                    links[0] = links[0] % RT + 1
                    ins.then_inc(rt, 1)
                    dve.wait_ge(rt, RT * step + links[0])

                def router():
                    links[0] = 0
                    dve.wait_ge(lg_ps, 4 * r + 4)
                    link(r, V.tensor_copy(lg[:].rearrange("p b e -> p (b e)"), pR[:, LOGITS:LOGITS + B * E]))
                    carry_wait(dve)
                    for b in range(B):
                        ins = V.max(mx[:, b], lg[:, b])
                    link(r, ins)
                    carry_wait(dve)
                    for b in range(B):
                        ins = V.max_index(ix[:, b], mx[:, b], lg[:, b])
                    V.tensor_tensor(pd[:, 0], mx[:, :, 1], mx[:, :, 0], ALU.subtract).then_inc(top_gap, 1)
                    link(r, ins)
                    link(r, V.tensor_copy(ixf[:], ix[:, :, 0:2]))
                    link(r, V.tensor_tensor(oh[:].rearrange("p b t e -> p (b t) e"),
                                            cfs[:, C_IOTA8:C_IOTA8 + E].unsqueeze(1).to_broadcast([P, 2 * B, E]),
                                            ixf[:].rearrange("p b t -> p (b t)").unsqueeze(2).to_broadcast([P, 2 * B, E]), ALU.is_equal))
                    V.tensor_tensor(cnt[:], oh[:, :, 0], oh[:, :, 1], ALU.add).then_inc(cnt_done, 1)

                def row_data():
                    links[0] = 5
                    V.tensor_copy(token_col[:, qp, :, TOKEN], cfs[:, bass.ds(q * B + C_TOKEN, B)])
                    V.tensor_copy(xn2[:, qp, :, FIRST], ixf[:, :, 0])
                    dve.wait_ge(top_exp, q + 1)
                    link(q, V.tensor_scalar(pd[:, 0], pd[:, 1], 1.0, None, ALU.add))
                    link(q, V.reciprocal(pd[:, 0], pd[:, 0]))
                    V.tensor_copy(xn2[:, qp, :, PROB1], pd[:, 0])
                    V.tensor_tensor(xn2[:, qp, :, PROB2], pd[:, 0], pd[:, 1], ALU.mult)

                def router_slots():
                    dve.wait_ge(pos_ps, q + 1)
                    caps = cfs[:, C_CAPS:C_CAPS + E].unsqueeze(1).to_broadcast([P, B, E])
                    link(q, V.tensor_tensor(pos[:], pR[:, POS:POS + B * E].rearrange("p (b e) -> p b e", b=B), caps, ALU.add))
                    link(q, V.tensor_tensor(sel[:], oh[:], pos[:].unsqueeze(2).to_broadcast([P, B, 2, E]), ALU.mult))
                    link(q, V.tensor_reduce(slf[:], sel[:].rearrange("p b t e -> p (b t) e"), AX.X, ALU.add))
                    if c >= 5:
                        dve.wait_ge(scat_out[qp], 128 * qh)
                    V.tensor_copy(cur[:, qp], slf[:]).then_inc(slot_done, 1)
                    with nc.allow_low_precision("counts up to 128 are exact in float16"):
                        link(q, V.tensor_reduce(ctmp[:], cnt[:].rearrange("p b e -> p e b"), AX.X, ALU.add))
                        V.tensor_tensor(carry[:], carry[:], ctmp[:], ALU.add).then_inc(carry_done, 1)
                    assert links[0] == RT, links

                def w1_low():
                    dve.wait_ge(w1_hi, i + 1)
                    V.scalar_tensor_tensor(w1s[:, 1, bass.ds(i, 1)].rearrange("p i f -> p (i f)"), w1raw[:], WS,
                                           w1s[:, 0, bass.ds(i, 1)].rearrange("p i f -> p (i f)"), ALU.mult, ALU.subtract).then_inc(w1_lo, 1)

                if fr:
                    x_lo(0)
                    x_lo(1)
                if c == 0:
                    for w in range(1, 4):
                        attention_weight(w)
                if bk:
                    score_lo(0, 0)
                if ro:
                    out_lo(r, 3)
                if ro:
                    residual(r, 2, c % 2)
                if bk:
                    score_lo(0, 1)
                if sc:
                    row_data()
                    router_slots()
                if bk:
                    score_lo(0, 2)
                if ro:
                    residual(r, 3, c % 2)
                    norm_moments(r, st2, mv2, ve2, (ln2_st, ln2_mv, ln2_ve))
                if bk:
                    score_lo(0, 3)
                    score_lo(1, 0)
                if fr and c >= 2:
                    w1_low()
                if bk:
                    attention(0)
                    state_part(0)
                if ro:
                    norm2_apply(0)
                if bk:
                    score_lo(1, 1)
                    out_lo(s, 0)
                    score_lo(1, 2)
                if ro:
                    norm2_apply(1)
                if c == STEPS + 1:
                    w2_low(0)
                    w2_low(1)
                if bk:
                    score_lo(1, 3)
                    residual(s, 0, sp_)
                    score_lo(2, 0)
                if nx:
                    norm1_stats(i + 1)
                if bk:
                    attention(1)
                    state_part(1)
                    score_lo(2, 1)
                if nx:
                    norm_moments(i + 1, st1, mv1, ve1, (ln1_st, ln1_mv, ln1_ve))
                if bk:
                    out_lo(s, 1)
                    score_lo(2, 2)
                    score_lo(2, 3)
                if fr:
                    values(0)
                if bk:
                    residual(s, 1, sp_)
                if nx:
                    norm1_shift(i + 1)
                if bk:
                    score_lo(3, 0)
                    score_lo(3, 1)
                    attention(2)
                    state_part(2)
                    score_lo(3, 2)
                    out_lo(s, 2)
                    score_lo(3, 3)
                if fr:
                    values(1)
                if ro:
                    router()
                if fr and c < 2:
                    w1_low()
                if bk:
                    attention(3)
                    state_part(3)
                if c == 0:
                    for n in range(2):
                        V.tensor_copy(pads[:].bitcast(I32)[:, n, TOKEN:TOKEN + 1], cfs[:, C_PAD + n:C_PAD + n + 1]).then_inc(pads_set, 1)

            norm1_stats(0)
            norm_moments(0, st1, mv1, ve1, (ln1_st, ln1_mv, ln1_ve))
            norm1_shift(0, first=True)
            dve.wait_ge(cf_in, 16)
            dve.wait_ge(consts_in, CONSTS)
            V.tensor_scalar(negb[:], bqks[:], -1.0, None, ALU.mult).then_inc(bias_prep, 1)
            V.tensor_scalar(linb[:], bqks[:], QS, None, ALU.mult).then_inc(bias_prep, 1)
            raw = kst[:].bitcast(F32).rearrange("p a b c -> p (a b c)")[:, 0:4 * KC * D].rearrange("p (w k n) -> p w k n", w=4, k=KC)

            def attention_weight(w):
                dve.wait_ge(wsplit_hi, w + 1)
                V.scalar_tensor_tensor(was[:, 1, w], raw[:, w], WS, was[:, 0, w], ALU.mult, ALU.subtract).then_inc(wsplit_lo, 1)

            attention_weight(0)
            V.memset(pads[:].rearrange("p s d -> p (s d)"), 0.0)
            def w2_low(n):
                dve.wait_ge(w2_hi, n + 1)
                lot = lambda x: x.rearrange("p e f d -> p (e f d)")
                V.scalar_tensor_tensor(lot(w2s[:, 1, n * W2E:(n + 1) * W2E]), lot(w2raw[:, n * W2E:(n + 1) * W2E]), WS,
                                       lot(w2s[:, 0, n * W2E:(n + 1) * W2E]), ALU.mult, ALU.subtract).then_inc(w2_lo, 1)

            iterations(dve, body)

            done = [0]

            def chain(ins):
                done[0] += 1
                ins.then_inc(tab, 1)
                dve.wait_ge(tab, done[0])

            dve.wait_ge(tot_ps, 1)
            caps = cfs[:, C_CAPS:C_CAPS + E]
            chain(V.tensor_copy(tiles_f[:, 0], pR[:, 0:E]))
            V.tensor_tensor(tails_i[:], tiles_f[0:1, 0], caps[0:1], ALU.add).then_inc(tail_done, 1)
            chain(V.tensor_scalar(tiles_i[:], tiles_f[:, 0], float(MT - 1), None, ALU.add))
            chain(V.tensor_scalar(tiles_i[:], tiles_i[:], int(math.log2(MT)), None, ALU.logical_shift_right))
            chain(V.tensor_copy(tiles_f[:, 1], tiles_i[:]))
            mine = tiles_f[:, 1]
            chain(V.tensor_tensor(upto, mine.unsqueeze(1).to_broadcast([P, E, E]),
                                  cfs[:, C_TRI8:C_TRI8 + E * E].rearrange("p (a b) -> p a b", a=E), ALU.mult))
            chain(V.tensor_reduce(tiles_f[:, 2], upto, AX.X, ALU.add))
            number = cfs[:, C_TILES:C_TILES + NT]
            chain(V.tensor_tensor(past, number.unsqueeze(2).to_broadcast([P, NT, E]),
                                  tiles_f[:, 2].unsqueeze(1).to_broadcast([P, NT, E]), ALU.is_ge))
            chain(V.tensor_reduce(tj[:, 0], past, AX.X, ALU.add))
            chain(V.tensor_tensor(past_tiles, past, mine.unsqueeze(1).to_broadcast([P, NT, E]), ALU.mult))
            chain(V.tensor_reduce(tj[:, 1], past_tiles, AX.X, ALU.add))
            chain(V.tensor_tensor(tj[:, 2], number, tj[:, 1], ALU.subtract))
            V.tensor_scalar(tile_expert[:], tj[:, 0], float(E - 1), None, ALU.min)
            chain(V.tensor_scalar(tj[:, 3], tj[:, 0], float(CAP), None, ALU.mult))
            chain(V.scalar_tensor_tensor(table[:, 0], tj[0:1, 2], float(MT), tj[0:1, 3], ALU.mult, ALU.add))
            chain(V.tensor_copy(table[:, 1], tile_expert[0:1]))
            assert done[0] == TAB, done

            for n in range(2, W2Q):
                w2_low(n)

            def tile(j, c):
                t, th = front_of(j, c)
                if is_tile(j, c + 2):
                    dve.wait_ge(gt_hi, t + 3)
                    V.tensor_tensor(gT[:, c % 2, 1], rows_T[c % 2][:], gT[:, c % 2, 0], ALU.subtract).then_inc(gt_lo, 1)
                if is_tile(j, c + 1):
                    p1 = (c + 1) % 2
                    dve.wait_ge(g_hi, t + 2)
                    V.tensor_tensor(ghl[:, p1, 1].rearrange("p f n -> p (f n)"), g[:, p1].rearrange("p f n -> p (f n)"),
                                    ghl[:, p1, 0].rearrange("p f n -> p (f n)"), ALU.subtract).then_inc(g_lo, 1)
                if is_tile(j, c + 2):
                    mine = tile_expert[:, bass.ds(t + 2, 1)]
                    dve.wait_ge(xg_in[c % 2], 16 * (j + (c + 2) // 2 + 1))
                    if c + 2 >= 1:
                        dve.wait_ge(meta, t + 2)
                    V.scalar_tensor_tensor(either[:, 0], xg[:, c % 2, :, FIRST], mine, xg[:, c % 2, :, PROB1], ALU.is_equal,
                                           ALU.mult).then_inc(which, 1)
                    V.scalar_tensor_tensor(either[:, 1], xg[:, c % 2, :, FIRST], mine, xg[:, c % 2, :, PROB2], ALU.not_equal,
                                           ALU.mult).then_inc(which, 1)
                    V.tensor_copy(row_token[:, bass.ds(t + 2, 1)].rearrange("p t s -> p (t s)"), xg[:].bitcast(I32)[:, c % 2, :, TOKEN])
                    dve.wait_ge(which, 2 * t + 6)
                    V.tensor_tensor(row_prob[:, bass.ds(t + 2, 1)].rearrange("p t s -> p (t s)"), either[:, 0], either[:, 1],
                                    ALU.add).then_inc(meta, 1)
                if is_tile(j, c):
                    e = dve.value_load(table[0:1, 1, bass.ds(t, 1)], min_val=0, max_val=E - 1)
                    dve.wait_ge(y_ps, t + 1)
                    if c == 0:
                        dve.wait_ge(b2_in, 16)
                    if c >= 2:
                        dve.wait_ge(added, 32 * (t - 1))
                    V.scalar_tensor_tensor(yt[:, c % 2], y_bank[c % 2][:].rearrange("p (s d) -> p s d", s=2), 1.0 / WS,
                                           b2s[:, bass.ds(e, 1)].to_broadcast([P, 2, D]), ALU.mult, ALU.add).then_inc(y_biased, 1)
                    dve.wait_ge(y_biased, t + 1)
                    for s in range(MT // P):
                        weight = row_prob[:, bass.ds(t, 1), s:s + 1].rearrange("p t s -> p (t s)")
                        V.tensor_scalar(yt[:, c % 2, s], yt[:, c % 2, s], weight, None, ALU.mult).then_inc(y_done, 1)

            tiles(dve, tile)

        @block.gpsimd
        def _(pool):
            G = nc.gpsimd
            pool.wait_ge(cf_in, 16)

            def rstd(i, ve, rs, made, done):
                pool.wait_ge(made, i + 1)
                G.tensor_tensor(rs[:], ve[:], cfs[:, C_POW:C_POW + B], ALU.pow).then_inc(done, 1)

            def add_bo(i, c):
                pool.wait_ge(xr_in, 16 * i + 16)
                G.tensor_tensor(xr[:, c % 2], xr[:, c % 2], bos[:].unsqueeze(1).to_broadcast([P, B, D]), ALU.add).then_inc(xr_done, 1)

            def body(j, c, front=True, back=True):
                i, _ = front_of(j, c)
                s, _ = front_of(j, c - 1)
                r, _ = front_of(j, c - 2)
                q, qh = front_of(j, c - 3)
                fr, bk, ro, sc = front and real(j, c), back and real(j, c - 1), real(j, c - 2), real(j, c - 3)
                nx = front and real(j, c + 1)
                par, sp_, qp = c % 2, (c - 1) % 2, (c - 3) % 2

                def feature(m):
                    pool.wait_ge(qk_neg, 8 * i + 2 * m + 2)
                    pool.wait_ge(qk_lin, 4 * i + m + 1)
                    if c >= 2 and m == 0:
                        pool.wait_ge(o_ps, 4 * (i - 1))
                    if c >= 1 and m == 2:
                        pool.wait_ge(kn_ps, 2 * i)
                    G.tensor_tensor(feature_rows(m, par), et[:, m % 2], lt[:, m % 2], ALU.add).then_inc(qk_f, 1)

                def low(m):
                    pool.wait_ge(qk_hi, 4 * i + m + 1)
                    G.tensor_tensor(qkhl[:, 1, m], feature_rows(m, par), qkhl[:, 0, m], ALU.subtract).then_inc(qk_lo, 1)

                def state_add(b):
                    g = 4 * s + b
                    pool.wait_ge(ut_done, g + 1)
                    pool.wait_ge(o_ps, g + 1)
                    sb_ = state[:, b].rearrange("p k n -> p (k n)")
                    G.tensor_tensor(sb_, sb_, ut[:], ALU.add).then_inc(state_new, 1)

                def scatter(b):
                    if b == 0:
                        pool.wait_ge(slot_done, q + 1)
                        carry_wait(pool)
                    for t in range(2):
                        G.indirect_dma_start(xg_dram, bass.IndirectOffsetOnAxis(ap=cur[:, qp, 2 * b + t:2 * b + t + 1], axis=0),
                                             xn2[:, qp, b], None).then_inc(scat_out[qp], 16)

                def v_low():
                    pool.wait_ge(v_hi, i + 1)
                    G.tensor_tensor(vhl[:, par, 1].rearrange("p b n -> p (b n)"), v[:, par].rearrange("p b h c -> p (b h c)"),
                                    vhl[:, par, 0].rearrange("p b n -> p (b n)"), ALU.subtract).then_inc(v_lo, 1)

                if nx and c < 2:
                    rstd(i + 1, ve1, rs1, ln1_ve, ln1_rs)
                if fr:
                    feature(0)
                if ro:
                    rstd(r, ve2, rs2, ln2_ve, ln2_rs)
                if fr:
                    feature(1)
                    low(0)
                    feature(2)
                    low(1)
                if bk:
                    state_add(0)
                if fr:
                    feature(3)
                    low(2)
                    low(3)
                if nx and c >= 2:
                    rstd(i + 1, ve1, rs1, ln1_ve, ln1_rs)
                if sc:
                    scatter(0)
                if bk:
                    state_add(1)
                if sc:
                    scatter(1)
                if fr:
                    add_bo(i, c)
                if sc:
                    scatter(2)
                if bk:
                    state_add(2)
                if sc:
                    scatter(3)
                if fr:
                    v_low()
                if bk:
                    state_add(3)

            rstd(0, ve1, rs1, ln1_ve, ln1_rs)
            for hf in range(2):
                G.memset(qst[:, hf].bitcast(F32).rearrange("p a b c -> p (a b c)"), 0.0).then_inc(qst_zero, 1)
            pool.wait_ge(consts_in, CONSTS)
            iterations(pool, body)

            def tile(j, c):
                t, _ = front_of(j, c)
                if not is_tile(j, c):
                    return
                if c == 0:
                    pool.wait_ge(x1_out, 16 * STEPS)
                    pool.wait_ge(pads_out, 16 * (E + 1))
                else:
                    pool.wait_ge(added, 32 * t)
                pool.wait_ge(meta, t + 1)
                G.tensor_copy(to_token[:, c % 2], row_token[:, bass.ds(t, 1)].rearrange("p t s -> p (t s)")).then_inc(token_copy, 1)
                pool.wait_ge(token_copy, t + 1)
                pool.wait_ge(y_done, 2 * t + 2)
                carry_wait(pool)
                for s in range(MT // P):
                    G.indirect_dma_start(out, bass.IndirectOffsetOnAxis(ap=to_token[:, c % 2, s:s + 1], axis=0), yt[:, c % 2, s],
                                         None, compute_op=ALU.add).then_inc(added, 16)

            pool.wait_ge(tab, TAB)
            tiles(pool, tile, 0)
            pool.wait_ge(added, 32 * NT)


def kernel(**inputs):
    import numpy as np
    import concourse.bacc as bacc
    from concourse.bass_utils import run_bass_kernel_spmd

    a = {k.split("_", 2)[2]: np.asarray(val) for k, val in inputs.items()}
    f, h, b = constants()
    data = {
        "x": a["x"].reshape(T, D),
        "wqkvo": np.stack([a["Wq"], a["Wk"], a["Wv"], a["Wo"]]),
        "bqk": np.concatenate([a["bq"], a["bk"]]).reshape(4, P).T,
        "bv": a["bv"].reshape(1, D),
        "bo": a["bo"].reshape(1, D),
        "rw": a["router_w"].T,
        "w1": a["w1"].reshape(E, F, KC, P).transpose(3, 0, 2, 1).reshape(P, E * KC * F),
        "b1": a["b1"].reshape(E * FC, P).T,
        "w2": a["w2"].reshape(E, D, FC, P).transpose(3, 0, 2, 1).reshape(P, E * FC * D),
        "b2": a["b2"].reshape(1, E * D),
        "cf": f,
        "ch": h,
        "cb": b.astype(mybir.dt.np(BF16)),
    }
    nc = bacc.Bacc("TRN2", target_bir_lowering=False, num_devices=1)
    arrays, args = {}, []
    for name, val in data.items():
        arrays[name] = np.ascontiguousarray(val)
        args.append(nc.dram_tensor(name, arrays[name].shape, mybir.dt.from_np(arrays[name].dtype), kind="ExternalInput").ap())
    args.append(nc.dram_tensor("out", (T + MT, D), F32, kind="ExternalOutput").ap())
    build(nc, *args)
    got = run_bass_kernel_spmd(nc, [arrays], core_ids=[0])
    return got.results[0]["out"][0:T].reshape(B, S, D)
```
